# Optimizing a Trainium2 kernel written in Bass

```python
import numpy as np
import jax
import jax.numpy as jnp

def _softmax(x, axis=-1):
    return jax.nn.softmax(x, axis=axis)

def _gelu(x):
    return jax.nn.gelu(x, approximate=True)

def _silu(x):
    return jax.nn.silu(x)

def _sigmoid(x):
    return jax.nn.sigmoid(x)

def _layernorm(x, axis=-1, eps=1e-05):
    m = jnp.mean(x, axis=axis, keepdims=True)
    v = jnp.var(x, axis=axis, keepdims=True)
    return (x - m) / jnp.sqrt(v + eps)

def _scatter_add(tgt, idx, src, axis=0):
    return tgt.at[idx].add(src)

def _segment_sum(src, seg, n):
    return jax.ops.segment_sum(src, seg, n)
kernel_name = 'mk_gnn_preln_d4_gnn_r64_cae7ed'

def setup_inputs(seed: int=0):
    np.random.seed(seed)
    _w = jnp.asarray

    def _rec_inputs():
        import jax
        import jax.numpy as jnp
        _gk = jax.random.key(seed)
        x = -0.0003713 + 1 * jax.random.normal(jax.random.fold_in(_gk, 1), (100000, 128), jnp.float32)
        src = jax.random.randint(jax.random.fold_in(_gk, 2), (50000,), 0, 100000, jnp.int32)
        dst = jnp.minimum((100000 * jax.random.uniform(jax.random.fold_in(_gk, 3), (50000,)) ** 2.0).astype(jnp.int32), 99999)
        _o = jnp.argsort(dst, stable=True)
        src = src[_o]
        dst = dst[_o]
        edge_attr_32 = -5.3897e-05 + 0.999841 * jax.random.normal(jax.random.fold_in(_gk, 12), (50000, 32), jnp.float32)
        edge_type_8 = jax.random.randint(jax.random.fold_in(_gk, 14), (50000,), 0, 8, jnp.int32)
        return (x, src, dst, edge_attr_32, edge_type_8)
    x, src, dst, edge_attr_32, edge_type_8 = _rec_inputs()

    def _L0_gnn_setup():
        import jax, jax.numpy as jnp
        import numpy as np
        N = 100000
        E = 25000
        D = 128
        key = jax.random.key(seed)
        k1, k2, k3, k4 = jax.random.split(key, 4)
        x = jax.random.normal(k1, (N, D), dtype=jnp.float32)
        row = jax.random.randint(k2, (E,), 0, N)
        off = jax.random.randint(k3, (E,), 1, N)
        col = (row + off) % N
        edge_index = jnp.stack([row, col]).astype(jnp.int64)
        std = float(np.sqrt(2.0 / (D + D)))
        W = jax.random.normal(k4, (D, D), dtype=jnp.float32) * std
        b = jnp.zeros((D,), dtype=jnp.float32)
        return {'x': x, 'edge_index': edge_index, 'W': W, 'b': b}
    _L0_gnn_all = _L0_gnn_setup()
    _L0_gnn_in = {k: v for k, v in _L0_gnn_all.items() if k in ('W', 'b')}
    del _L0_gnn_all

    def _L1_gnn_setup():
        import jax, jax.numpy as jnp
        import numpy as np
        N_NODES = 50000
        N_EDGES = 500000
        IN_DIM = 128
        OUT_DIM = 128
        N_REL = 8
        key = jax.random.key(seed)
        k1, k2, k3, k4 = jax.random.split(key, 4)
        x = jax.random.normal(k1, (N_NODES, IN_DIM), dtype=jnp.float32)
        limit = float(np.sqrt(6.0 / (IN_DIM + OUT_DIM)))
        weight = jax.random.uniform(k2, (N_REL, IN_DIM, OUT_DIM), dtype=jnp.float32, minval=-limit, maxval=limit)
        bias = jnp.zeros((OUT_DIM,), dtype=jnp.float32)
        edge_index = jax.random.randint(k3, (2, N_EDGES), 0, N_NODES, dtype=jnp.int64)
        edge_type = jax.random.randint(k4, (N_EDGES,), 0, N_REL, dtype=jnp.int64)
        return {'x': x, 'weight': weight, 'bias': bias, 'edge_index': edge_index, 'edge_type': edge_type}
    _L1_gnn_all = _L1_gnn_setup()
    _L1_gnn_in = {k: v for k, v in _L1_gnn_all.items() if k in ('weight', 'bias')}
    del _L1_gnn_all

    def _L2_gnn_setup():
        import jax, jax.numpy as jnp
        import numpy as np
        N_NODES = 50000
        NUM_FEATURES = 128
        HIDDEN = 128
        OUT = 64
        N_EDGES = 9375

        def gcn_conv(x, edge_index, W, b, n_nodes):
            xw = x @ W
            loop = jnp.arange(n_nodes, dtype=edge_index.dtype)
            row = jnp.concatenate([edge_index[0], loop])
            col = jnp.concatenate([edge_index[1], loop])
            ones = jnp.ones(row.shape[0], dtype=xw.dtype)
            deg = jax.ops.segment_sum(ones, col, num_segments=n_nodes)
            dis = jnp.where(deg > 0, jax.lax.rsqrt(deg), 0.0)
            norm = dis[row] * dis[col]
            msg = xw[row] * norm[:, None]
            agg = jax.ops.segment_sum(msg, col, num_segments=n_nodes)
            return agg + b
        key = jax.random.key(seed)
        ks = jax.random.split(key, 10)
        x = jax.random.normal(ks[0], (N_NODES, NUM_FEATURES), dtype=jnp.float32)
        edge_index = jax.random.randint(ks[1], (2, N_EDGES), 0, N_NODES, dtype=jnp.int64)
        s1 = 1.0 / np.sqrt(NUM_FEATURES)
        s2 = 1.0 / np.sqrt(HIDDEN)
        s3 = 1.0 / np.sqrt(OUT)
        W_enc1 = jax.random.uniform(ks[2], (NUM_FEATURES, HIDDEN), jnp.float32, -s1, s1)
        b_enc1 = jnp.zeros((HIDDEN,), jnp.float32)
        W_enc2 = jax.random.uniform(ks[3], (HIDDEN, OUT), jnp.float32, -s2, s2)
        b_enc2 = jnp.zeros((OUT,), jnp.float32)
        W_dec1 = jax.random.uniform(ks[4], (OUT, HIDDEN), jnp.float32, -s3, s3)
        b_dec1 = jax.random.uniform(ks[5], (HIDDEN,), jnp.float32, -s3, s3)
        W_dec2 = jax.random.uniform(ks[6], (HIDDEN, NUM_FEATURES), jnp.float32, -s2, s2)
        b_dec2 = jax.random.uniform(ks[7], (NUM_FEATURES,), jnp.float32, -s2, s2)
        return {'x': x, 'edge_index': edge_index, 'W_enc1': W_enc1, 'b_enc1': b_enc1, 'W_enc2': W_enc2, 'b_enc2': b_enc2, 'W_dec1': W_dec1, 'b_dec1': b_dec1, 'W_dec2': W_dec2, 'b_dec2': b_dec2}
    _L2_gnn_all = _L2_gnn_setup()
    _L2_gnn_in = {k: v for k, v in _L2_gnn_all.items() if k in ('W_enc1', 'b_enc1', 'W_enc2', 'b_enc2', 'W_dec1', 'b_dec1', 'W_dec2', 'b_dec2')}
    del _L2_gnn_all

    def _L3_gnn_setup():
        import jax, jax.numpy as jnp
        import numpy as np
        N_NODES = 50000
        N_EDGES = 12500
        IN_DIM_N = 128
        IN_DIM_E = 32
        OUT_DIM = 128
        key = jax.random.key(seed)
        k = jax.random.split(key, 6)
        nfeats = jax.random.normal(k[0], (N_NODES, IN_DIM_N), dtype=jnp.float32)
        efeats = jax.random.normal(k[1], (N_EDGES, IN_DIM_E), dtype=jnp.float32)
        W_fc = jax.random.normal(k[2], (OUT_DIM, IN_DIM_N), dtype=jnp.float32) * (2.0 / np.sqrt(IN_DIM_N + OUT_DIM))
        W_attn = jax.random.normal(k[3], (1, 2 * OUT_DIM + IN_DIM_E), dtype=jnp.float32) * 0.08
        src = jax.random.randint(k[4], (N_EDGES,), 0, N_NODES, dtype=jnp.int32)
        dst = jax.random.randint(k[5], (N_EDGES,), 0, N_NODES, dtype=jnp.int32)
        return {'nfeats': nfeats, 'efeats': efeats, 'W_fc': W_fc, 'W_attn': W_attn, 'src': src, 'dst': dst}
    _L3_gnn_all = _L3_gnn_setup()
    _L3_gnn_in = {k: v for k, v in _L3_gnn_all.items() if k in ('W_fc', 'W_attn')}
    del _L3_gnn_all
    return {'x': x, 'src': src, 'dst': dst, 'edge_attr_32': edge_attr_32, 'edge_type_8': edge_type_8, 'L0_gnn_W': _L0_gnn_in['W'], 'L0_gnn_b': _L0_gnn_in['b'], 'L1_gnn_weight': _L1_gnn_in['weight'], 'L1_gnn_bias': _L1_gnn_in['bias'], 'L2_gnn_W_enc1': _L2_gnn_in['W_enc1'], 'L2_gnn_b_enc1': _L2_gnn_in['b_enc1'], 'L2_gnn_W_enc2': _L2_gnn_in['W_enc2'], 'L2_gnn_b_enc2': _L2_gnn_in['b_enc2'], 'L2_gnn_W_dec1': _L2_gnn_in['W_dec1'], 'L2_gnn_b_dec1': _L2_gnn_in['b_dec1'], 'L2_gnn_W_dec2': _L2_gnn_in['W_dec2'], 'L2_gnn_b_dec2': _L2_gnn_in['b_dec2'], 'L3_gnn_W_fc': _L3_gnn_in['W_fc'], 'L3_gnn_W_attn': _L3_gnn_in['W_attn']}

def reference(x, src, dst, edge_attr_32, edge_type_8, L0_gnn_W, L0_gnn_b, L1_gnn_weight, L1_gnn_bias, L2_gnn_W_enc1, L2_gnn_b_enc1, L2_gnn_W_enc2, L2_gnn_b_enc2, L2_gnn_W_dec1, L2_gnn_b_dec1, L2_gnn_W_dec2, L2_gnn_b_dec2, L3_gnn_W_fc, L3_gnn_W_attn):
    import jax
    import jax.numpy as jnp

    def _L0_gnn_ref(x, edge_index, W, b):
        import jax, jax.numpy as jnp
        import numpy as np
        N = 100000
        E = 25000
        D = 128
        n = x.shape[0]
        loops = jnp.arange(n, dtype=edge_index.dtype)
        row = jnp.concatenate([edge_index[0], loops])
        col = jnp.concatenate([edge_index[1], loops])
        deg = jax.ops.segment_sum(jnp.ones(row.shape[0], dtype=x.dtype), row, num_segments=n)
        dis = deg ** (-0.5)
        norm = dis[row] * dis[col]
        xj = x[col] * norm[:, None]
        agg = jax.ops.segment_sum(xj, row, num_segments=n)
        out = jax.nn.relu(agg @ W.T + b)
        return x + out

    def _L1_gnn_ref(x, weight, bias, edge_index, edge_type):
        import jax, jax.numpy as jnp
        import numpy as np
        N_NODES = 50000
        N_EDGES = 500000
        IN_DIM = 128
        OUT_DIM = 128
        N_REL = 8
        src = edge_index[0]
        dst = edge_index[1]
        xw = jnp.einsum('ni,rio->rno', x, weight)
        msgs = jax.nn.relu(xw[edge_type, src] + bias)
        out = jax.ops.segment_sum(msgs, dst, num_segments=x.shape[0])
        return out

    def _L2_gnn_ref(x, edge_index, W_enc1, b_enc1, W_enc2, b_enc2, W_dec1, b_dec1, W_dec2, b_dec2):
        import jax, jax.numpy as jnp
        import numpy as np
        N_NODES = 50000
        NUM_FEATURES = 128
        HIDDEN = 128
        OUT = 64
        N_EDGES = 9375

        def gcn_conv(x, edge_index, W, b, n_nodes):
            xw = x @ W
            loop = jnp.arange(n_nodes, dtype=edge_index.dtype)
            row = jnp.concatenate([edge_index[0], loop])
            col = jnp.concatenate([edge_index[1], loop])
            ones = jnp.ones(row.shape[0], dtype=xw.dtype)
            deg = jax.ops.segment_sum(ones, col, num_segments=n_nodes)
            dis = jnp.where(deg > 0, jax.lax.rsqrt(deg), 0.0)
            norm = dis[row] * dis[col]
            msg = xw[row] * norm[:, None]
            agg = jax.ops.segment_sum(msg, col, num_segments=n_nodes)
            return agg + b
        n = x.shape[0]
        z = jax.nn.relu(gcn_conv(x, edge_index, W_enc1, b_enc1, n))
        z = jax.nn.relu(gcn_conv(z, edge_index, W_enc2, b_enc2, n))
        z = jax.nn.relu(z @ W_dec1 + b_dec1)
        x_hat = z @ W_dec2 + b_dec2
        return x_hat

    def _L3_gnn_ref(nfeats, efeats, W_fc, W_attn, src, dst):
        import jax, jax.numpy as jnp
        import numpy as np
        N_NODES = 50000
        N_EDGES = 12500
        IN_DIM_N = 128
        IN_DIM_E = 32
        OUT_DIM = 128
        n_nodes = nfeats.shape[0]
        out_dim = W_fc.shape[0]
        in_dim_e = efeats.shape[1]
        z = nfeats @ W_fc.T
        a = W_attn[0]
        a_src = a[:out_dim]
        a_e = a[out_dim:out_dim + in_dim_e]
        a_dst = a[out_dim + in_dim_e:]
        s_src = z @ a_src
        s_dst = z @ a_dst
        s_e = efeats @ a_e
        e = jax.nn.leaky_relu(s_src[src] + s_e + s_dst[dst], negative_slope=0.01)
        m = jax.ops.segment_max(e, dst, num_segments=n_nodes)
        m = jnp.where(jnp.isfinite(m), m, 0.0)
        w = jnp.exp(e - m[dst])
        denom = jax.ops.segment_sum(w, dst, num_segments=n_nodes)
        alpha = w / jnp.where(denom > 0, denom, 1.0)[dst]
        h = jax.ops.segment_sum(alpha[:, None] * z[src], dst, num_segments=n_nodes)
        return h
    edge_index = jnp.stack([src, dst])
    h = jnp.maximum(_layernorm(x, axis=-1), 0.0)
    x = x + _L0_gnn_ref(h, edge_index, L0_gnn_W, L0_gnn_b)
    h = jnp.maximum(_layernorm(x, axis=-1), 0.0)
    x = x + _L1_gnn_ref(h, L1_gnn_weight, L1_gnn_bias, edge_index, edge_type_8)
    h = jnp.maximum(_layernorm(x, axis=-1), 0.0)
    x = x + _L2_gnn_ref(h, edge_index, L2_gnn_W_enc1, L2_gnn_b_enc1, L2_gnn_W_enc2, L2_gnn_b_enc2, L2_gnn_W_dec1, L2_gnn_b_dec1, L2_gnn_W_dec2, L2_gnn_b_dec2)
    h = jnp.maximum(_layernorm(x, axis=-1), 0.0)
    x = x + _L3_gnn_ref(h, edge_attr_32, L3_gnn_W_fc, L3_gnn_W_attn, src, dst)
    return x

_drawn_inputs = setup_inputs


def setup_inputs(seed=0):
    import zlib

    import numpy as np

    out = dict(_drawn_inputs(seed))
    spreads = {'L0_gnn_b': (0.0, 0.1),
     'L1_gnn_bias': (0.0, 0.328),
     'L2_gnn_b_enc1': (0.0, 0.8),
     'L2_gnn_b_enc2': (0.0, 0.8)}
    factors = {'edge_attr_32': 3.67,
     'L2_gnn_W_enc1': 5.26,
     'L2_gnn_W_enc2': 4.312,
     'L2_gnn_W_dec1': 3.668,
     'L2_gnn_b_dec1': 3.882,
     'L2_gnn_b_dec2': 3.213}
    for name, (base, spread) in spreads.items():
        noise = np.random.default_rng([zlib.crc32(name.encode()), seed]).standard_normal(out[name].shape)
        drawn = base * np.exp(spread * noise) if base else spread * noise
        out[name] = jnp.asarray(drawn.astype(out[name].dtype))
    for name, factor in factors.items():
        out[name] = (out[name] * factor).astype(out[name].dtype)
    return out
```

```python
import concourse.bass as bass
from concourse import mybir
from contextlib import ExitStack

F32 = mybir.dt.float32
F16 = mybir.dt.float16
I32 = mybir.dt.int32
ALU = mybir.AluOpType
ACT = mybir.ActivationFunctionType
AX = mybir.AxisListType

N, E, D, H2, DE, R = 100000, 50000, 128, 64, 32, 8
P = 128
EPS = 1e-5
BIG = 1e30
ROUND = 1.5 * 2 ** 23

K = 10
BR = P * K
NB = N // BR
PT = (N - NB * BR) // K
NC = (NB + 1) * K
SLOTS = 3
assert NB % SLOTS == 0 and PT * K + NB * BR == N

T = 392
LASTP = E // T
LASTN = E - LASTP * T
NPAIR = T // 2
RING = 4
AHEAD = 2
TX = T + 2 * AHEAD
NR = N + 2 * P
EXTRA = {"ring": AHEAD, "kt": 1, "xt": 1, "xtc": 1, "xw": 2}
assert LASTP == P - 1 and NPAIR % RING == 0


def needed(count):
    return not isinstance(count, int) or count > 0


class Count:
    def __init__(self, sem, base):
        self.sem, self.base = sem, base

    def after(self, n):
        return self.base + n


def rounds(eng, body, per_round, count):
    for u in range(per_round):
        body(0, u)
    with eng.Fori(1, count // per_round) as r:
        for u in range(per_round):
            body(r, u)


def node_loop(eng, first, second=None, lag=1):
    def body(r, u, p=P):
        first(r, u, p)
        if second is not None and not (isinstance(r, int) and r * SLOTS + u < lag):
            if u >= lag:
                second(r, u - lag, P)
            else:
                second(r - 1, u - lag + SLOTS, P)
    rounds(eng, body, SLOTS, NB)
    body(NB // SLOTS, 0, PT)
    if second is not None:
        for b in range(NB + 1 - lag, NB + 1):
            second(b // SLOTS, b % SLOTS, PT if b == NB else P)


def gnn(nc, x, src, dst, ea, et, w_l0, b_l0, w_l1, b_l1, we1, be1, we2, be2, wd1, bd1, wd2, bd2,
        w_fc, w_at, out):
    with ExitStack() as ctx:
        def sb(name, shape, dt=F32):
            return ctx.enter_context(nc.sbuf_tensor(name, shape, dt))

        def dram(name, shape):
            return nc.dram_tensor(name, shape, F32, kind="Internal").ap()

        made = {}

        def phase(family, per, counts, slotted=None):
            def count(name, total):
                sem, base = made.get(f"{family}_{name}") or (ctx.enter_context(nc.semaphore(f"{family}_{name}")), 0)
                made[f"{family}_{name}"] = sem, base + total
                return Count(sem, base)
            names = {}
            for n in counts.split():
                name, _, times = n.partition(":")
                names[name] = count(name, per * int(times or 1) + EXTRA.get(name, 0) * (family == "edge"))
            for name, totals in (slotted or {}).items():
                names[name] = [count(f"{name}{i}", n) for i, n in enumerate(totals)]
            return names

        t_src = dram("t_src", (N, D))
        t_acc = dram("t_acc", (NR, D))
        t_x = dram("t_x", (NR, D))
        t_y = dram("t_y", (N, H2))
        t_yacc = dram("t_yacc", (NR, H2))
        t_h3 = dram("t_h3", (N, D + 1))
        t_sd = dram("t_sd", (N, 1))
        t_me = dram("t_me", (TX, P, D))

        ps = ctx.enter_context(nc.psum_tensor("ps", [P, 4096], F32))

        ident = sb("ident", [P, P])
        ones = sb("ones", [P, P])
        ioc = sb("ioc", [P, NC], F16)
        iop = sb("iop", [P, P], F16)
        earlier = sb("earlier", [P, 2, 2 * P])
        spare = sb("spare", [P, 2])
        zero = sb("zero", [P, 2 * D])
        iot = sb("iot", [P, R])
        w0t = sb("w0t", [D, D])
        wn = sb("wn", [D, D])
        w1 = sb("w1", [D, R, D])
        we1s = sb("we1s", [D, D])
        we2s = sb("we2s", [D, H2])
        wd1s = sb("wd1s", [P, 2, D])
        wd2s = sb("wd2s", [D, D])
        wfn = sb("wfn", [D, D])
        wft = sb("wft", [D, D])
        acol = sb("acol", [D, 2])
        vs = sb("vs", [D, 2])
        b0b = sb("b0b", [P, D])
        b1b = sb("b1b", [P, D])
        bd2b = sb("bd2b", [P, D])
        aeb = sb("aeb", [P, DE])
        be1c = sb("be1c", [D, 1])
        be2c = sb("be2c", [2 * H2, 1])
        bd1c = sb("bd1c", [D, 1])

        src_i = sb("src_i", [P, TX], I32)
        dst_i = sb("dst_i", [P, TX], I32)
        typ_i = sb("typ_i", [P, TX], I32)
        src_f = sb("src_f", [P, TX])
        dst_f = sb("dst_f", [P, TX])
        typ_f = sb("typ_f", [P, TX])
        hcol = [sb(f"hcol{i}", [P, T]) for i in range(2)]
        hpar = [sb(f"hpar{i}", [P, T]) for i in range(2)]
        ta = sb("ta", [P, T])
        tb = sb("tb", [P, T])
        tcv = sb("tcv", [P, T])
        dis = [sb("dis_src", [P, NC]), sb("dis_dst", [P, NC])]
        mean_r = sb("mean_r", [P, NC])
        rstd_r = sb("rstd_r", [P, NC])

        gidx = sb("gidx", [P, RING, 2], I32)
        didx = sb("didx", [P, RING, 2], I32)
        sidx = sb("sidx", [P, RING, 2], I32)
        keyr = sb("keyr", [P, RING, 2])
        keyd = sb("keyd", [P, RING, 2])
        typr = sb("typr", [P, RING, 2])
        alr = sb("alr", [P, RING, 2])
        tmask = sb("tmask", [P, 2, 2, R])
        cnt = sb("cnt", [P, 2, 2])
        mdup = sb("mdup", [P, 2, 2])
        seq = sb("seq", [P, 2, 2, 2 * P])
        junk = sb("junk", [P, 2, 2 * P])
        g = sb("g", [P, RING, 2, D + 1])
        gd = sb("gd", [P, RING, 2])
        tot = sb("tot", [P, RING, 2, D])
        msg = sb("msg", [P, 2, 2, D])
        sel = sb("sel", [P, 2, 2, 2, D])
        toty = sb("toty", [P, RING, 2, H2])
        xT = sb("xT", [P, 2, 2, D])
        oneh_p = sb("oneh_p", [P, 2, P], F16)
        oneh_c = sb("oneh_c", [P, 2, NC], F16)

        KD = K * D
        dense = sb("dense", [P, 9 * KD])

        def area(n):
            return dense[:, n * KD:(n + 1) * KD].rearrange("p (k f) -> p k f", k=K)
        xin = [area(i) for i in range(3)]
        ain = [area(3 + i) for i in range(3)]
        oa = [area(6 + i) for i in range(3)]
        yin = [dense[:, (3 + i) * KD:(3 + i) * KD + K * H2].rearrange("p (k f) -> p k f", k=K) for i in range(3)]
        yout = [dense[:, (6 + i) * KD:(6 + i) * KD + K * H2].rearrange("p (k f) -> p k f", k=K) for i in range(3)]
        hb = [sb(f"hb{i}", [P, K, D]) for i in range(3)]
        ob = [sb(f"ob{i}", [P, K, D + 1]) for i in range(3)]
        tT = sb("tT", [P, K, P])
        fT = sb("fT", [P, K, P])
        ob_h = [sb(f"ob_h{i}", [P, K, D]) for i in range(3)]
        hT = sb("hT", [P, K, P])
        dz = sb("dz", [P, SLOTS, K])
        col2 = sb("col2", [P, 4])
        SUMS = 2 * 512
        ZC = 3 * 512
        zc_view = ps[:, ZC:ZC + KD].rearrange("f (k p) -> f k p", k=K)
        HG = [(0, 3), (3, 6), (6, 9), (9, K)]
        SCOL = 7 * 512 + 3 * P
        NLD = 18
        NDEG = 22
        row = sb("row", [1, 16, P])
        TURNS = "row row row col row row col row col row row col".split()
        names = {n: row[0:1, j, :] for j, n in enumerate(
            ("first", "last", "contp", "contn", "single", "t", "neg", "scan", "cinn", "dn", "base", "turn", "turned"))}
        sdb = sb("sdb", [P, SLOTS, K])
        st = sb("st", [P, K, 6])
        mv = sb("mv", [P, K, 2])
        var = sb("var", [P, K])
        std = sb("std", [P, K])
        rs = sb("rs", [P, K])
        sc = sb("sc", [P, SLOTS, K])
        nbi = sb("nbi", [P, SLOTS, K])
        sc2 = sb("sc2", [P, SLOTS, K])
        nb2 = sb("nb2", [P, SLOTS, K])
        dsl = sb("dsl", [P, SLOTS, K])
        EH = T // 4
        eas = [dense[:, i * EH * DE:(i + 1) * EH * DE].rearrange("p (t d) -> p t d", d=DE) for i in range(2)]
        prod = dense[:, 2 * EH * DE:3 * EH * DE].rearrange("p (t d) -> p t d", d=DE)
        e_ = sb("e_", [P, TX])
        se = sb("se", [P, T])
        fwd = sb("fwd", [P, T])
        bwd = sb("bwd", [P, T])
        same = sb("same", [P, T])
        nsame = sb("nsame", [P, T])
        gsame = sb("gsame", [P, T])
        gnot = sb("gnot", [P, T])
        wgt = sb("wgt", [P, T])
        alpha = sb("alpha", [P, TX])
        col = sb("col", [P, 12])

        gate = ctx.enter_context(nc.semaphore("phase_done"))
        tick = ctx.enter_context(nc.semaphore("pool_tick"))
        phases = [0, 0, 0, 0, 0]
        block = ctx.enter_context(nc.Block())

        def end_phase(eng, who):
            phases[who] += 1
            eng.drain().then_inc(gate, 1)
            eng.wait_ge(gate, 5 * phases[who])

        SP, AC, VE, PE, PO = range(5)

        def rows_of(table, b, p):
            return table[bass.ds(b * BR, p * K), :].rearrange("(p k) f -> p k f", k=K)

        def slots(n):
            return [n * len(range(u, NB + 1, SLOTS)) for u in range(SLOTS)]

        S0 = phase("setup", 1, "ld lde zero pad made calc deg hot mm root")
        LN = "copy bn mv var std rs sc "
        A0 = phase("node", NB + 1, LN + "nb h", {"ld": slots(16), "sto": slots(32)})
        EN = "ring kt s cnt mdup sidx mm tot scat:32 "
        GA = {"gath": [32 * NPAIR // RING + 32 * (u < AHEAD) for u in range(RING)]}
        E0 = phase("edge", NPAIR, EN, GA)
        L0 = phase("node", NB + 1, LN + "nb:2 h tr trc mm z xh res h1",
                   {"ld": slots(16), "lda": slots(16), "sto": slots(32)})
        E1 = phase("edge", NPAIR, EN + f"xt xtc xw:2 mask sel:{2 * (R + 1)} relu", GA)
        A2 = phase("node", NB + 1, LN + "nb h", {"ld": slots(16), "sto": slots(32)})
        E2 = phase("edge", NPAIR, EN, GA)
        L2 = phase("node", NB + 1, "copy scal tr trc mm relu mm2 y", {"ld": slots(16), "sto": slots(32)})
        E3 = phase("edge", NPAIR, EN, GA)
        L3 = phase("node", NB + 1, LN + "nb scal tr trc d1 d1c d2 xb x3 h3 ht:4 htc:4 s so",
                   {"ld": slots(16), "lda": slots(16), "sto": slots(48)})
        A3 = phase("scores", NPAIR, "ring e", {"gath": [0] * RING, "sto": [0] * RING})
        M3 = phase("softmax", 1, "v ready pe ex diff exp", {"ld": [0] * 4})
        B3 = phase("edge", NPAIR, EN + "mul sums ttc tt fin", {"load": [0] * RING})

        def edge_pool(gp, s, table, width, target):
            def gath(q, u):
                gp.wait_ge(s["ring"].sem, s["ring"].after(q + 1))
                gp.sem_inc(tick, 1)
                for c in range(2):
                    gp.indirect_dma_start(g[:, u, c, 0:width], None, table,
                                          bass.IndirectOffsetOnAxis(ap=gidx[:, u, c:c + 1], axis=0)) \
                        .then_inc(s["gath"][u].sem, 16)
            if table is not None:
                for q in range(AHEAD):
                    gath(q, q)

            def body(r, u):
                q = r * RING + u
                if table is not None:
                    gath(q + AHEAD, (u + AHEAD) % RING)
                gp.wait_ge(s["sidx"].sem, s["sidx"].after(q + 1))
                gp.sem_inc(tick, 1)
                gp.wait_ge(s["tot"].sem, s["tot"].after(q + 1))
                gp.sem_inc(tick, 1)
                if needed(q * 32):
                    gp.wait_ge(s["scat"].sem, s["scat"].after(q * 32))
                    gp.sem_inc(tick, 1)
                for c in range(2):
                    gp.indirect_dma_start(target, bass.IndirectOffsetOnAxis(ap=sidx[:, u, c:c + 1], axis=0),
                                          tot_of(target)[:, u, c, :], None, compute_op=ALU.add).then_inc(s["scat"].sem, 16)
            rounds(gp, body, RING, NPAIR)
            if table is not None:
                for a in range(AHEAD):
                    gp.wait_ge(s["gath"][a].sem, s["gath"][a].after(32 * (NPAIR // RING + 1)))
            gp.wait_ge(s["scat"].sem, s["scat"].after(32 * NPAIR))

        def tot_of(target):
            return tot if target.shape[1] == D else toty

        def edge_vector(v, s, gi, key, more=None, between=None):
            def ring(q, u):
                if needed((q - RING + 1) * 32):
                    v.wait_ge(s["scat"].sem, s["scat"].after((q - RING + 1) * 32))
                nc.vector.tensor_scalar(gidx[:, u, :], gi[:, bass.ds(q * 2, 2)], 1.0, None, ALU.mult)
                if more is not None:
                    more(q, u)
                nc.vector.tensor_scalar(keyr[:, u, :], key[:, bass.ds(q * 2, 2)], 1.0, None, ALU.mult) \
                    .then_inc(s["ring"].sem, 1)
            for q in range(AHEAD):
                ring(q, q)

            def body(r, u):
                q, w = r * RING + u, u % 2
                ring(q + AHEAD, (u + AHEAD) % RING)
                v.wait_ge(s["kt"].sem, s["kt"].after(q + 1))
                if needed(q - 1):
                    v.wait_ge(s["mm"].sem, s["mm"].after(q - 1))
                for c in range(2):
                    i = nc.vector.tensor_scalar(seq[:, w, c, :], ps[:, 0:2 * P], keyr[:, u, c:c + 1],
                                                None, ALU.is_equal)
                i.then_inc(s["s"].sem, 1)
                if between is not None:
                    between(v, r, u)
                v.wait_ge(s["s"].sem, s["s"].after(q + 1))
                nc.vector.tensor_tensor(keyd[:, u, :], spare[:, :], keyr[:, u, :], ALU.subtract)
                for c in range(2):
                    i = nc.vector.tensor_tensor_reduce(out=junk[:, c, :], in0=seq[:, w, c, :], in1=earlier[:, c, :],
                                                       scale=1.0, scalar=0.0, op0=ALU.mult, op1=ALU.add,
                                                       accum_out=cnt[:, w, c:c + 1])
                i.then_inc(s["cnt"].sem, 1)
                v.wait_ge(s["cnt"].sem, s["cnt"].after(q + 1))
                nc.vector.scalar_tensor_tensor(out=mdup[:, w, :], in0=cnt[:, w, :], scalar=1.0, in1=keyd[:, u, :],
                                               op0=ALU.min, op1=ALU.mult).then_inc(s["mdup"].sem, 1)
                v.wait_ge(s["mdup"].sem, s["mdup"].after(q + 1))
                nc.vector.tensor_tensor(sidx[:, u, :], mdup[:, w, :], keyr[:, u, :], ALU.add).then_inc(s["sidx"].sem, 1)
            rounds(v, body, RING, NPAIR)

        def edge_tensor(pe, s, width, rows_ready, rows, prepare=None, after=None):
            def keys(q, u):
                pe.wait_ge(s["ring"].sem, s["ring"].after(q + 1))
                if needed(q):
                    pe.wait_ge(s["s"].sem, s["s"].after(q))
                for c in range(2):
                    i = nc.tensor.transpose(ps[:, c * P:(c + 1) * P], keyr[:, u, c:c + 1].to_broadcast([P, P]), ident[:, :])
                i.then_inc(s["kt"].sem, 1)
            keys(0, 0)
            if prepare is not None:
                prepare(pe, 0, 0)

            def body(r, u):
                q, w = r * RING + u, u % 2
                r1, u1 = (r, u + 1) if u + 1 < RING else (r + 1, 0)
                keys(q + 1, u1)
                if prepare is not None:
                    prepare(pe, r1, u1)
                pe.wait_ge(s["s"].sem, s["s"].after(q + 1))
                rows_ready(pe, r, u)
                if needed(q - 1):
                    pe.wait_ge(s["tot"].sem, s["tot"].after(q - 1))
                for d in range(2):
                    o = SUMS + w * 512 + d * P
                    for c in range(2):
                        i = nc.tensor.matmul(ps[:, o:o + width], seq[:, w, c, d * P:(d + 1) * P],
                                             rows[:, u % rows.shape[1], c, 0:width], start=(c == 0), stop=(c == 1))
                i.then_inc(s["mm"].sem, 1)
                if after is not None:
                    after(pe, r, u)
            rounds(pe, body, RING, NPAIR)

        def gathered(s):
            def ready(pe, r, u):
                pe.wait_ge(s["gath"][u].sem, s["gath"][u].after(r * 32 + 32))
            return ready

        def pair_sums(w, width):
            return ps[:, SUMS + w * 512:SUMS + w * 512 + 256].rearrange("p (c f) -> p c f", c=2)[:, :, 0:width]

        def edge_scalar(a, s, width, t_out):
            def body(r, u):
                q = r * RING + u
                if needed((q - RING + 1) * 32):
                    a.wait_ge(s["scat"].sem, s["scat"].after((q - RING + 1) * 32))
                a.wait_ge(s["mm"].sem, s["mm"].after(q + 1))
                nc.scalar.activation(t_out[:, u, :, :], pair_sums(u % 2, width), ACT.Copy).then_inc(s["tot"].sem, 1)
            rounds(a, body, RING, NPAIR)

        def stats(v, s, b, u, p, xt, d_src):
            for k in range(K):
                i = nc.vector.bn_stats(st[0:p, k, :], xt[0:p, k, :])
            i.then_inc(s["bn"].sem, 1)
            v.wait_ge(s["bn"].sem, s["bn"].after(b + 1))
            nc.vector.tensor_scalar(dsl[0:p, u, :], d_src[0:p, bass.ds(b * K, K)], 1.0, None, ALU.mult) \
                .then_inc(s["copy"].sem, 1)
            for k in range(K):
                i = nc.vector.bn_aggr(mv[0:p, k, :], st[0:p, k, :])
            i.then_inc(s["mv"].sem, 1)
            v.wait_ge(s["mv"].sem, s["mv"].after(b + 1))
            nc.vector.tensor_scalar(var[0:p, :], mv[0:p, :, 1], EPS, None, ALU.add).then_inc(s["var"].sem, 1)
            v.wait_ge(s["std"].sem, s["std"].after(b + 1))
            nc.vector.reciprocal(rs[0:p, :], std[0:p, :]).then_inc(s["rs"].sem, 1)
            v.wait_ge(s["rs"].sem, s["rs"].after(b + 1))

        def root(a, s, b, p):
            a.wait_ge(s["var"].sem, s["var"].after(b + 1))
            nc.scalar.activation(std[0:p, :], var[0:p, :], ACT.Sqrt).then_inc(s["std"].sem, 1)

        def relu_rows(a, p, out_t, in_t, scale, bias):
            for k in range(K):
                i = nc.scalar.activation(out_t[0:p, k, 0:D], in_t[0:p, k, :], ACT.Relu, bias=bias[0:p, k:k + 1],
                                         scale=scale[0:p, k:k + 1])
            return i

        def ln_sync(sp, s, table):
            def load(r, u, p):
                b = r * SLOTS + u
                if needed(b - SLOTS + 1):
                    sp.wait_ge(s["h"].sem, s["h"].after(b - SLOTS + 1))
                sp.dma_start(xin[u][0:p], rows_of(table, b, p)).then_inc(s["ld"][u].sem, 16)

            def store(r, u, p):
                b = r * SLOTS + u
                sp.wait_ge(s["h"].sem, s["h"].after(b + 1))
                sp.dma_start(rows_of(t_src, b, p), oa[u][0:p]).then_inc(s["sto"][u].sem, 16)
                sp.dma_start(rows_of(t_acc, b, p), oa[u][0:p]).then_inc(s["sto"][u].sem, 16)
            node_loop(sp, load, store, 2)
            stored(sp, s, 32)

        def stored(sp, s, per):
            for u in range(SLOTS):
                sp.wait_ge(s["sto"][u].sem, s["sto"][u].after(per * len(range(u, NB + 1, SLOTS))))

        def ln_vector(v, s, d_src, keep):
            def body(r, u, p):
                b = r * SLOTS + u
                v.wait_ge(s["ld"][u].sem, s["ld"][u].after(r * 16 + 16))
                stats(v, s, b, u, p, xin[u], d_src)
                nc.vector.tensor_tensor(sc[0:p, u, :], rs[0:p, :], dsl[0:p, u, :], ALU.mult).then_inc(s["sc"].sem, 1)
                if keep:
                    nc.vector.tensor_scalar(rstd_r[0:p, bass.ds(b * K, K)], rs[0:p, :], 1.0, None, ALU.mult)
                    nc.vector.scalar_tensor_tensor(out=mean_r[0:p, bass.ds(b * K, K)], in0=mv[0:p, :, 0], scalar=-1.0,
                                                   in1=rs[0:p, :], op0=ALU.mult, op1=ALU.mult)
                v.wait_ge(s["sc"].sem, s["sc"].after(b + 1))
                nc.vector.scalar_tensor_tensor(out=nbi[0:p, u, :], in0=mv[0:p, :, 0], scalar=-1.0, in1=sc[0:p, u, :],
                                               op0=ALU.mult, op1=ALU.mult).then_inc(s["nb"].sem, 1)
            node_loop(v, body)

        def ln_scalar(a, s):
            def first(r, u, p):
                root(a, s, r * SLOTS + u, p)

            def body(r, u, p):
                b = r * SLOTS + u
                root(a, s, b, p)
                if needed(r * 32):
                    a.wait_ge(s["sto"][u].sem, s["sto"][u].after(r * 32))
                a.wait_ge(s["nb"].sem, s["nb"].after(b + 1))
                relu_rows(a, p, oa[u], xin[u], sc[:, u, :], nbi[:, u, :]).then_inc(s["h"].sem, 1)
            node_loop(a, body)

        @block.sync
        def _(sp):
            sp.dma_start(wn[:, :], w_l0).then_inc(S0["ld"].sem, 16)
            sp.dma_start(w1[:, :, :], w_l1.rearrange("r i o -> i r o")).then_inc(S0["ld"].sem, 16)
            sp.dma_start(we1s[:, :], we1).then_inc(S0["ld"].sem, 16)
            sp.dma_start(we2s[:, :], we2).then_inc(S0["ld"].sem, 16)
            for h in range(2):
                sp.dma_start(be2c[h * H2:(h + 1) * H2, :], be2.rearrange("(p a) -> p a", a=1)).then_inc(S0["ld"].sem, 16)
            sp.dma_start(wd2s[:, :], wd2).then_inc(S0["ld"].sem, 16)
            sp.dma_start(wfn[:, :], w_fc).then_inc(S0["ld"].sem, 16)
            with nc.allow_non_contiguous_dma(reason="vectors to partitions, once"):
                sp.dma_start(acol[:, 0:1], w_at[0, 0:D].rearrange("(p a) -> p a", a=1)).then_inc(S0["ld"].sem, 16)
                sp.dma_start(acol[:, 1:2], w_at[0, D + DE:2 * D + DE].rearrange("(p a) -> p a", a=1)).then_inc(S0["ld"].sem, 16)
            sp.dma_start(be1c[:, :], be1.rearrange("(p a) -> p a", a=1)).then_inc(S0["ld"].sem, 16)
            sp.dma_start(bd1c[:, :], bd1.rearrange("(p a) -> p a", a=1)).then_inc(S0["ld"].sem, 16)
            for row_t, bias in ((b0b, b_l0), (b1b, b_l1), (bd2b, bd2)):
                sp.dma_start(row_t[:, :], bias.rearrange("(a n) -> a n", a=1).to_broadcast([P, D])).then_inc(S0["ld"].sem, 16)
            sp.dma_start(aeb[:, :], w_at[0:1, D:D + DE].to_broadcast([P, DE])).then_inc(S0["ld"].sem, 16)
            sp.wait_ge(S0["pad"].sem, S0["pad"].after(1))
            for h in range(2):
                sp.dma_start(wd1s[h * H2:(h + 1) * H2, h, :], wd1).then_inc(S0["ld"].sem, 16)
            for idx, arr in ((src_i, src), (dst_i, dst), (typ_i, et)):
                sp.dma_start(idx[0:LASTP, 0:T], arr[0:LASTP * T].rearrange("(p t) -> p t", t=T)).then_inc(S0["lde"].sem, 16)
                sp.dma_start(idx[LASTP:P, 0:LASTN], arr[LASTP * T:E].rearrange("(p t) -> p t", p=1)).then_inc(S0["lde"].sem, 16)
            for table in (t_acc, t_x, out):
                sp.dma_start(table[N:NR, :].rearrange("(p c) f -> p (c f)", c=2), zero[:, :]).then_inc(S0["zero"].sem, 16)
            sp.dma_start(t_yacc[N:NR, :].rearrange("(p c) f -> p (c f)", c=2), zero[:, 0:D]).then_inc(S0["zero"].sem, 16)
            sp.wait_ge(S0["zero"].sem, S0["zero"].after(16 * 4))
            sp.wait_ge(S0["ld"].sem, S0["ld"].after(16 * NLD))
            sp.wait_ge(S0["lde"].sem, S0["lde"].after(16 * 6))
            end_phase(sp, SP)
            ln_sync(sp, A0, x)
            end_phase(sp, SP)
            end_phase(sp, SP)

            def conv0_load(r, u, p):
                b = r * SLOTS + u
                if needed(b - SLOTS + 1):
                    sp.wait_ge(L0["xh"].sem, L0["xh"].after(b - SLOTS + 1))
                sp.dma_start(xin[u][0:p], rows_of(x, b, p)).then_inc(L0["ld"][u].sem, 16)
                if needed(b - SLOTS + 1):
                    sp.wait_ge(L0["tr"].sem, L0["tr"].after(b - SLOTS + 1))
                sp.dma_start(ain[u][0:p], rows_of(t_acc, b, p)).then_inc(L0["lda"][u].sem, 16)

            def conv0_store(r, u, p):
                b = r * SLOTS + u
                sp.wait_ge(L0["h1"].sem, L0["h1"].after(b + 1))
                sp.dma_start(rows_of(t_x, b, p), oa[u][0:p]).then_inc(L0["sto"][u].sem, 16)
                sp.dma_start(rows_of(t_src, b, p), hb[u][0:p]).then_inc(L0["sto"][u].sem, 16)
            node_loop(sp, conv0_load, conv0_store, 2)
            stored(sp, L0, 32)
            end_phase(sp, SP)
            end_phase(sp, SP)
            ln_sync(sp, A2, t_x)
            end_phase(sp, SP)
            end_phase(sp, SP)

            def enc_load(r, u, p):
                b = r * SLOTS + u
                if needed(b - SLOTS + 1):
                    sp.wait_ge(L2["tr"].sem, L2["tr"].after(b - SLOTS + 1))
                sp.dma_start(ain[u][0:p], rows_of(t_acc, b, p)).then_inc(L2["ld"][u].sem, 16)

            def enc_store(r, u, p):
                b = r * SLOTS + u
                sp.wait_ge(L2["y"].sem, L2["y"].after(b + 1))
                sp.dma_start(rows_of(t_y, b, p), yout[u][0:p]).then_inc(L2["sto"][u].sem, 16)
                sp.dma_start(rows_of(t_yacc, b, p), yout[u][0:p]).then_inc(L2["sto"][u].sem, 16)
            node_loop(sp, enc_load, enc_store, 2)
            stored(sp, L2, 32)
            end_phase(sp, SP)
            end_phase(sp, SP)

            def dec_load(r, u, p):
                b = r * SLOTS + u
                if needed(b - SLOTS + 1):
                    sp.wait_ge(L3["x3"].sem, L3["x3"].after(b - SLOTS + 1))
                sp.dma_start(xin[u][0:p], rows_of(t_x, b, p)).then_inc(L3["ld"][u].sem, 16)
                if needed(b - SLOTS + 1):
                    sp.wait_ge(L3["tr"].sem, L3["tr"].after(b - SLOTS + 1))
                sp.dma_start(yin[u][0:p], rows_of(t_yacc, b, p)).then_inc(L3["lda"][u].sem, 16)

            def dec_store(r, u, p):
                b = r * SLOTS + u
                sp.wait_ge(L3["so"].sem, L3["so"].after(b + 1))
                sp.dma_start(rows_of(out, b, p), oa[u][0:p]).then_inc(L3["sto"][u].sem, 16)
                sp.dma_start(rows_of(t_h3, b, p), ob[u][0:p]).then_inc(L3["sto"][u].sem, 16)
                sp.dma_start(t_sd[bass.ds(b * BR, p * K), :].rearrange("(p k) f -> p (k f)", k=K), sdb[0:p, u, :]) \
                    .then_inc(L3["sto"][u].sem, 16)
            node_loop(sp, dec_load, dec_store, 2)
            stored(sp, L3, 48)
            end_phase(sp, SP)

            def keep_rows(r, u):
                q = r * RING + u
                sp.wait_ge(A3["gath"][u].sem, A3["gath"][u].after(r * 64 + 64))
                sp.dma_start(t_me[bass.ds(q * 2, 2), :, :].rearrange("c p f -> p c f"), g[:, u, :, 0:D]) \
                    .then_inc(A3["sto"][u].sem, 16)
            rounds(sp, keep_rows, RING, NPAIR)
            for u in range(RING):
                sp.wait_ge(A3["sto"][u].sem, A3["sto"][u].after(16 * NPAIR // RING))
            end_phase(sp, SP)

            for i in range(4):
                if needed(i - 1):
                    sp.wait_ge(M3["ex"].sem, M3["ex"].after(i - 1))
                sp.dma_start(eas[i % 2][0:LASTP], ea[0:LASTP * T, :].rearrange("(p t) d -> p t d", t=T)
                             [:, i * EH:(i + 1) * EH, :]).then_inc(M3["ld"][i].sem, 16)
                n = min(max(LASTN - i * EH, 0), EH)
                if n:
                    lo = LASTP * T + i * EH
                    sp.dma_start(eas[i % 2][LASTP:P, 0:n, :], ea[lo:lo + n, :].rearrange("(p t) d -> p t d", p=1)) \
                        .then_inc(M3["ld"][i].sem, 16)
                sp.wait_ge(M3["ld"][i].sem, M3["ld"][i].after(32 if n else 16))
            end_phase(sp, SP)

            def load_rows(r, u):
                q = r * RING + u
                if needed((q - RING + 1) * 32):
                    sp.wait_ge(B3["scat"].sem, B3["scat"].after((q - RING + 1) * 32))
                for c in range(2):
                    sp.dma_start(g[:, u, c, 0:D], t_me[bass.ds(q * 2 + c, 1), :, :].rearrange("c p f -> p (c f)")) \
                        .then_inc(B3["load"][u].sem, 16)
            rounds(sp, load_rows, RING, NPAIR)
            end_phase(sp, SP)

        @block.gpsimd
        def _(gp):
            gp.memset(ident[:, :], 0.0).then_inc(S0["made"].sem, 1)
            gp.memset(ones[:, :], 1.0).then_inc(S0["made"].sem, 1)
            gp.memset(earlier[:, :, :], 1.0).then_inc(S0["made"].sem, 1)
            gp.memset(zero[:, :], 0.0)
            gp.memset(wd1s[:, :, :], 0.0)
            gp.memset(src_i[:, :], 0)
            gp.memset(dst_i[:, :], 0)
            gp.memset(typ_i[:, :], 0).then_inc(S0["pad"].sem, 1)
            gp.iota(ioc[:, :], [[1, NC]], base=0, channel_multiplier=0, allow_small_or_imprecise_dtypes=True)
            gp.iota(iop[:, :], [[1, P]], base=0, channel_multiplier=0, allow_small_or_imprecise_dtypes=True)
            gp.iota(iot[:, :], [[1, R]], base=0, channel_multiplier=0, allow_small_or_imprecise_dtypes=True)
            gp.iota(spare[:, :], [[P, 2]], base=N, channel_multiplier=1, allow_small_or_imprecise_dtypes=True)
            gp.wait_ge(S0["made"].sem, S0["made"].after(3))
            gp.affine_select(out=ident[:, :], in_=ident[:, :], compare_op=ALU.not_equal, fill=1.0, base=0,
                             pattern=[[-1, P]], channel_multiplier=1)
            i = gp.affine_select(out=earlier[:, :, :], in_=earlier[:, :, :], compare_op=ALU.is_gt, fill=0.0, base=0,
                                 pattern=[[P, 2], [-1, 2 * P]], channel_multiplier=1)
            i.then_inc(S0["made"].sem, 1)
            gp.wait_ge(S0["calc"].sem, S0["calc"].after(1))
            for f in (src_f, dst_f):
                i = gp.affine_select(out=f[:, 0:T], in_=f[:, 0:T], compare_op=ALU.is_ge, fill=float(N + LASTP), base=E - 1,
                                     pattern=[[-1, T]], channel_multiplier=-T)
            i.then_inc(S0["made"].sem, 1)
            end_phase(gp, PO)
            end_phase(gp, PO)
            edge_pool(gp, E0, t_src, D, t_acc)
            end_phase(gp, PO)

            def conv0_xh(r, u, p):
                b = r * SLOTS + u
                gp.wait_ge(L0["h"].sem, L0["h"].after(b + 1))
                gp.tensor_tensor(ob_h[u][0:p], xin[u][0:p], ob_h[u][0:p], ALU.add).then_inc(L0["xh"].sem, 1)
            node_loop(gp, conv0_xh)
            end_phase(gp, PO)
            edge_pool(gp, E1, t_src, D, t_x)
            end_phase(gp, PO)
            end_phase(gp, PO)
            edge_pool(gp, E2, t_src, D, t_acc)
            end_phase(gp, PO)
            end_phase(gp, PO)
            edge_pool(gp, E3, t_y, H2, t_yacc)
            end_phase(gp, PO)

            def dec_xb(r, u, p):
                b = r * SLOTS + u
                gp.wait_ge(L3["ld"][u].sem, L3["ld"][u].after(r * 16 + 16))
                gp.tensor_tensor(xin[u][0:p], xin[u][0:p], bd2b[0:p, :].rearrange("p (a f) -> p a f", a=1)
                                 .to_broadcast([p, K, D]), ALU.add).then_inc(L3["xb"].sem, 1)
            node_loop(gp, dec_xb)
            end_phase(gp, PO)

            def edge_rows(r, u):
                gp.wait_ge(A3["ring"].sem, A3["ring"].after(r * RING + u + 1))
                gp.sem_inc(tick, 1)
                for c in range(2):
                    gp.indirect_dma_start(g[:, u, c, :], None, t_h3,
                                          bass.IndirectOffsetOnAxis(ap=gidx[:, u, c:c + 1], axis=0)) \
                        .then_inc(A3["gath"][u].sem, 16)
                    gp.indirect_dma_start(gd[:, u, c:c + 1], None, t_sd,
                                          bass.IndirectOffsetOnAxis(ap=didx[:, u, c:c + 1], axis=0)) \
                        .then_inc(A3["gath"][u].sem, 16)
            rounds(gp, edge_rows, RING, NPAIR)
            end_phase(gp, PO)
            end_phase(gp, PO)
            edge_pool(gp, B3, None, D, out)
            end_phase(gp, PO)

        def softmax(v):
            n_v, turn = [0], [0]

            def link(i):
                n_v[0] += 1
                i.then_inc(M3["v"].sem, 1)
                v.wait_ge(M3["v"].sem, M3["v"].after(n_v[0]))
            vec = nc.vector
            link(vec.memset(alpha[:, :], 0.0))
            link(vec.memset(se[:, :], 0.0))
            for i in range(4):
                n = min(max(LASTN - i * EH, 0), EH)
                v.wait_ge(M3["ld"][i].sem, M3["ld"][i].after(32 if n else 16))
                link(vec.tensor_tensor(prod[0:LASTP], eas[i % 2][0:LASTP], aeb[0:LASTP, :].rearrange("p (a d) -> p a d", a=1)
                                       .to_broadcast([LASTP, EH, DE]), ALU.mult))
                link(vec.tensor_reduce(se[0:LASTP, i * EH:(i + 1) * EH], prod[0:LASTP], AX.X, ALU.add))
                if n:
                    link(vec.tensor_tensor(prod[96:P, 0:n], eas[i % 2][96:P, 0:n], aeb[96:P, :]
                                           .rearrange("p (a d) -> p a d", a=1).to_broadcast([P - 96, n, DE]), ALU.mult))
                    link(vec.tensor_reduce(se[96:P, i * EH:i * EH + n], prod[96:P, 0:n], AX.X, ALU.add))
                v.sem_inc(M3["ex"].sem, 1)
            link(vec.tensor_tensor(se[:, :], se[:, :], e_[:, 0:T], ALU.add))
            link(vec.scalar_tensor_tensor(out=e_[:, 0:T], in0=se[:, :], scalar=0.01, in1=se[:, :], op0=ALU.mult, op1=ALU.max))
            link(vec.memset(same[:, :], 1.0))
            link(vec.memset(gsame[:, :], 1.0))
            link(vec.tensor_tensor(same[:, 1:T], dst_f[:, 1:T], dst_f[:, 0:T - 1], ALU.is_equal))
            link(vec.tensor_scalar(gsame[:, 0:T - 1], same[:, 1:T], 1.0, None, ALU.mult))
            link(vec.tensor_scalar(nsame[:, :], same[:, :], -1.0, BIG, ALU.add, ALU.mult))
            link(vec.tensor_scalar(gnot[:, :], gsame[:, :], -1.0, 1.0, ALU.mult, ALU.add))
            def row_step(name, column):
                n = turn[0]
                assert TURNS[n] == "row"
                turn[0] += 1
                vec.tensor_copy(col[:, n:n + 1], column).then_inc(M3["ready"].sem, 1)
                v.wait_ge(M3["pe"].sem, M3["pe"].after(n + 1))
                link(vec.tensor_copy(names[name], ps[0:1, 0:P]))

            def col_step(column):
                n = turn[0]
                assert TURNS[n] == "col"
                turn[0] += 1
                vec.tensor_copy(names["turned"], names["turn"]).then_inc(M3["ready"].sem, 1)
                v.wait_ge(M3["pe"].sem, M3["pe"].after(n + 1))
                link(vec.tensor_copy(column, ps[:, 0:1]))
            row_step("first", dst_f[:, 0:1])
            row_step("last", dst_f[:, T - 1:T])
            R_ = names
            link(vec.memset(R_["contp"], 0.0))
            link(vec.memset(R_["contn"], 0.0))
            link(vec.tensor_tensor(R_["contp"][:, 1:P], R_["first"][:, 1:P], R_["last"][:, 0:P - 1], ALU.is_equal))
            link(vec.tensor_tensor(R_["contn"][:, 0:P - 1], R_["first"][:, 1:P], R_["last"][:, 0:P - 1], ALU.is_equal))
            link(vec.tensor_tensor(R_["single"], R_["first"], R_["last"], ALU.is_equal))
            link(vec.tensor_scalar(R_["cinn"], R_["contp"], -1.0, BIG, ALU.add, ALU.mult))

            def back_fill(values, out_t):
                link(vec.tensor_tensor(tcv[:, :], gnot[:, :], values, ALU.mult))
                link(vec.tensor_scalar(ta[:, :], gsame[:, :], 1.0, None, ALU.mult))
                link(vec.memset(ta[:, T - 1:T], 0.0))
                link(vec.tensor_scalar(tcv[:, T - 1:T], values[:, T - 1:T], 1.0, None, ALU.mult))
                link(vec.tensor_tensor_scan(out_t[:, ::-1], ta[:, ::-1], tcv[:, ::-1], 0.0, ALU.mult, ALU.add))
                row_step("t", out_t[:, 0:1])
                row_step("base", values[:, T - 1:T])
                link(vec.tensor_tensor(R_["dn"], R_["single"], R_["contn"], ALU.mult))
                link(vec.tensor_scalar(R_["turn"], R_["dn"], -1.0, 1.0, ALU.mult, ALU.add))
                link(vec.tensor_tensor(R_["turn"], R_["turn"], R_["t"], ALU.mult))
                link(vec.tensor_tensor_scan(R_["scan"][:, ::-1], R_["dn"][:, ::-1], R_["turn"][:, ::-1], 0.0, ALU.mult, ALU.add))
                link(vec.tensor_scalar(R_["turn"], R_["contn"], -1.0, 1.0, ALU.mult, ALU.add))
                link(vec.tensor_tensor(R_["turn"], R_["turn"], R_["base"], ALU.mult))
                link(vec.tensor_tensor(R_["neg"][:, 0:P - 1], R_["contn"][:, 0:P - 1], R_["scan"][:, 1:P], ALU.mult))
                link(vec.tensor_tensor(R_["turn"][:, 0:P - 1], R_["turn"][:, 0:P - 1], R_["neg"][:, 0:P - 1], ALU.add))
                col_step(col2[:, 0:1])
                link(vec.tensor_tensor(tcv[:, :], gnot[:, :], values, ALU.mult))
                link(vec.tensor_tensor_scan(out_t[:, ::-1], gsame[:, ::-1], tcv[:, ::-1], col2[:, 0:1], ALU.mult, ALU.add))

            link(vec.tensor_scalar(tb[:, :], nsame[:, :], 1.0, None, ALU.mult))
            link(vec.memset(tb[:, 0:1], 0.0))
            link(vec.tensor_tensor_scan(fwd[:, :], tb[:, :], e_[:, 0:T], -BIG, ALU.add, ALU.max))
            row_step("t", fwd[:, T - 1:T])
            link(vec.tensor_tensor(R_["dn"], R_["single"], R_["contp"], ALU.mult))
            link(vec.tensor_scalar(R_["dn"], R_["dn"], -1.0, BIG, ALU.add, ALU.mult))
            link(vec.tensor_tensor_scan(R_["scan"], R_["dn"], R_["t"], -BIG, ALU.add, ALU.max))
            link(vec.memset(R_["turn"], -BIG))
            link(vec.tensor_tensor(R_["turn"][:, 1:P], R_["scan"][:, 0:P - 1], R_["cinn"][:, 1:P], ALU.add))
            col_step(col2[:, 1:2])
            link(vec.tensor_tensor_scan(fwd[:, :], tb[:, :], e_[:, 0:T], col2[:, 1:2], ALU.add, ALU.max))
            back_fill(fwd[:, :], bwd)
            vec.tensor_tensor(wgt[:, :], e_[:, 0:T], bwd[:, :], ALU.subtract).then_inc(M3["diff"].sem, 1)
            v.wait_ge(M3["exp"].sem, M3["exp"].after(1))
            link(vec.tensor_scalar(tb[:, :], same[:, :], 1.0, None, ALU.mult))
            link(vec.tensor_tensor_scan(fwd[:, :], tb[:, :], wgt[:, :], 0.0, ALU.mult, ALU.add))
            row_step("t", fwd[:, T - 1:T])
            link(vec.tensor_tensor(R_["dn"], R_["single"], R_["contp"], ALU.mult))
            link(vec.tensor_tensor_scan(R_["scan"], R_["dn"], R_["t"], 0.0, ALU.mult, ALU.add))
            link(vec.memset(R_["turn"], 0.0))
            link(vec.tensor_tensor(R_["turn"][:, 1:P], R_["scan"][:, 0:P - 1], R_["contp"][:, 1:P], ALU.mult))
            col_step(col2[:, 2:3])
            link(vec.tensor_tensor_scan(fwd[:, :], tb[:, :], wgt[:, :], col2[:, 2:3], ALU.mult, ALU.add))
            back_fill(fwd[:, :], bwd)
            link(vec.tensor_scalar(ta[:, :], bwd[:, :], 0.0, None, ALU.is_le))
            link(vec.tensor_tensor(bwd[:, :], bwd[:, :], ta[:, :], ALU.add))
            link(vec.reciprocal(bwd[:, :], bwd[:, :]))
            link(vec.tensor_tensor(alpha[:, 0:T], wgt[:, :], bwd[:, :], ALU.mult))

        @block.vector
        def _(v):
            done = [0]

            def link(i, sem=S0["deg"]):
                done[0] += 1
                i.then_inc(sem.sem, 1)
                v.wait_ge(sem.sem, sem.after(done[0]))

            v.wait_ge(S0["lde"].sem, S0["lde"].after(16 * 6))
            for f, i32 in ((src_f, src_i), (dst_f, dst_i), (typ_f, typ_i)):
                i = nc.vector.tensor_copy(f[:, :], i32[:, :])
            i.then_inc(S0["calc"].sem, 1)
            v.wait_ge(S0["made"].sem, S0["made"].after(5))
            for f, hp, hc in ((src_f, hpar[0], hcol[0]), (dst_f, hpar[1], hcol[1])):
                def floor_div(out_t, in_t, n):
                    link(nc.vector.tensor_scalar(out_t, in_t, 1.0 / n, 0.5 / n - 0.5, ALU.mult, ALU.add))
                    link(nc.vector.tensor_scalar(out_t, out_t, ROUND, None, ALU.add))
                    link(nc.vector.tensor_scalar(out_t, out_t, -ROUND, None, ALU.add))
                floor_div(ta[:, :], f[:, 0:T], BR)
                link(nc.vector.scalar_tensor_tensor(out=tb[:, :], in0=ta[:, :], scalar=-float(BR), in1=f[:, 0:T],
                                                    op0=ALU.mult, op1=ALU.add))
                floor_div(hp[:, :], tb[:, :], K)
                link(nc.vector.scalar_tensor_tensor(out=tb[:, :], in0=hp[:, :], scalar=-float(K), in1=tb[:, :],
                                                    op0=ALU.mult, op1=ALU.add))
                link(nc.vector.scalar_tensor_tensor(out=hc[:, :], in0=ta[:, :], scalar=float(K), in1=tb[:, :],
                                                    op0=ALU.mult, op1=ALU.add))
            for n in range(2):
                def hot(r, u):
                    t = r * 4 + u
                    if needed(t - 1 + n * T):
                        v.wait_ge(S0["mm"].sem, S0["mm"].after(t - 1 + n * T))
                    nc.vector.tensor_scalar(oneh_p[:, u % 2, :], iop[:, :], hpar[n][:, bass.ds(t, 1)], None, ALU.is_equal)
                    nc.vector.tensor_scalar(oneh_c[:, u % 2, :], ioc[:, :], hcol[n][:, bass.ds(t, 1)], None, ALU.is_equal) \
                        .then_inc(S0["hot"].sem, 1)
                rounds(v, hot, 4, T)
            v.wait_ge(S0["mm"].sem, S0["mm"].after(2 * T))
            for n in range(2):
                for j in range(2):
                    lo = j * NC // 2
                    link(nc.vector.tensor_scalar(dis[n][:, lo:lo + NC // 2], ps[:, (2 * n + j) * 512:(2 * n + j) * 512 + NC // 2],
                                                 1.0, None, ALU.add))
            nc.vector.tensor_copy(w0t[:, :], ps[:, 2048:2048 + D])
            nc.vector.tensor_copy(wft[:, :], ps[:, 2048 + D:2048 + 2 * D])
            nc.vector.tensor_copy(vs[:, :], ps[:, 2048 + 2 * D:2048 + 2 * D + 2])
            v.wait_ge(S0["root"].sem, S0["root"].after(1))
            for n in range(2):
                link(nc.vector.reciprocal(dis[n][:, :], dis[n][:, :]))
            end_phase(v, VE)
            ln_vector(v, A0, dis[0], True)
            end_phase(v, VE)
            edge_vector(v, E0, dst_i, src_f)
            end_phase(v, VE)

            def conv0_slot(r, u, p):
                b = r * SLOTS + u
                if needed(b - SLOTS + 1):
                    v.wait_ge(L0["h"].sem, L0["h"].after(b - SLOTS + 1))
                for slot, kept in ((sc, rstd_r), (nbi, mean_r)):
                    i = nc.vector.tensor_scalar(slot[0:p, u, :], kept[0:p, bass.ds(b * K, K)], 1.0, None, ALU.mult)
                i.then_inc(L0["sc"].sem, 1)

            def conv0_rest(r, u, p):
                b = r * SLOTS + u
                if needed(r * 32):
                    v.wait_ge(L0["sto"][u].sem, L0["sto"][u].after(r * 32))
                nc.vector.tensor_scalar(dz[0:p, u, :], dis[0][0:p, bass.ds(b * K, K)], 1.0, None, ALU.mult) \
                    .then_inc(L0["nb"].sem, 1)
                v.wait_ge(L0["nb"].sem, L0["nb"].after(b * 2 + 1))
                v.wait_ge(L0["mm"].sem, L0["mm"].after(b + 1))
                for k in range(K):
                    i = nc.vector.scalar_tensor_tensor(out=oa[u][0:p, k, :], in0=ps[0:p, ZC + k * P:ZC + (k + 1) * P],
                                                       scalar=dz[0:p, u, k:k + 1], in1=b0b[0:p, :], op0=ALU.mult,
                                                       op1=ALU.add)
                i.then_inc(L0["z"].sem, 1)
                v.wait_ge(L0["z"].sem, L0["z"].after(b + 1))
                v.wait_ge(L0["xh"].sem, L0["xh"].after(b + 1))
                nc.vector.scalar_tensor_tensor(out=oa[u][0:p], in0=oa[u][0:p], scalar=0.0, in1=ob_h[u][0:p],
                                               op0=ALU.max, op1=ALU.add).then_inc(L0["res"].sem, 1)
                v.wait_ge(L0["res"].sem, L0["res"].after(b + 1))
                stats(v, L0, b, u, p, oa[u], dis[0])
                nc.vector.tensor_scalar(sc2[0:p, u, :], rs[0:p, :], 1.0, None, ALU.mult)
                nc.vector.scalar_tensor_tensor(out=nb2[0:p, u, :], in0=mv[0:p, :, 0], scalar=-1.0, in1=rs[0:p, :],
                                               op0=ALU.mult, op1=ALU.mult).then_inc(L0["nb"].sem, 1)
            node_loop(v, conv0_slot, conv0_rest)
            end_phase(v, VE)

            def type_ring(q, u):
                nc.vector.tensor_scalar(typr[:, u, :], typ_f[:, bass.ds(q * 2, 2)], 1.0, None, ALU.mult)

            def select(v, r, u):
                q, w = r * RING + u, u % 2
                for c in range(2):
                    i = nc.vector.tensor_scalar(tmask[:, w, c, :], iot[:, :], typr[:, u, c:c + 1], None, ALU.is_equal)
                i.then_inc(E1["mask"].sem, 1)
                v.wait_ge(E1["mask"].sem, E1["mask"].after(q + 1))
                if needed(q - 1):
                    v.wait_ge(E1["relu"].sem, E1["relu"].after(q - 1))
                for c in range(2):
                    v.wait_ge(E1["xw"].sem, E1["xw"].after(q * 2 + c + 1))
                    for k in range(R):
                        if k >= 2:
                            v.wait_ge(E1["sel"].sem, E1["sel"].after(q * 2 * (R + 1) + c * (R + 1) + k - 1))
                        o = 2048 + c * 1024 + k * P
                        part = sel[:, w, c, k % 2, :]
                        if k == 1:
                            i = nc.vector.tensor_scalar(part, ps[:, o:o + D], tmask[:, w, c, k:k + 1], None, ALU.mult)
                        else:
                            i = nc.vector.scalar_tensor_tensor(out=part, in0=ps[:, o:o + D], scalar=tmask[:, w, c, k:k + 1],
                                                               in1=b1b[:, :] if k == 0 else part, op0=ALU.mult,
                                                               op1=ALU.add)
                        i.then_inc(E1["sel"].sem, 1)
                    v.wait_ge(E1["sel"].sem, E1["sel"].after(q * 2 * (R + 1) + c * (R + 1) + R))
                    nc.vector.tensor_tensor(sel[:, w, c, 0, :], sel[:, w, c, 0, :], sel[:, w, c, 1, :], ALU.add) \
                        .then_inc(E1["sel"].sem, 1)
            edge_vector(v, E1, src_i, dst_f, type_ring, select)
            end_phase(v, VE)
            ln_vector(v, A2, dis[1], False)
            end_phase(v, VE)
            edge_vector(v, E2, src_i, dst_f)
            end_phase(v, VE)

            def enc_scale(r, u, p):
                b = r * SLOTS + u
                if needed(b - SLOTS + 1):
                    v.wait_ge(L2["y"].sem, L2["y"].after(b - SLOTS + 1))
                nc.vector.tensor_scalar(dsl[0:p, u, :], dis[1][0:p, bass.ds(b * K, K)], 1.0, None, ALU.mult) \
                    .then_inc(L2["copy"].sem, 1)
                v.wait_ge(L2["copy"].sem, L2["copy"].after(b + 1))
                v.wait_ge(L2["ld"][u].sem, L2["ld"][u].after(r * 16 + 16))
                nc.vector.tensor_tensor(ain[u][0:p], ain[u][0:p], norm_of(u, p, D), ALU.mult).then_inc(L2["scal"].sem, 1)

            def norm_of(u, p, width):
                return dsl[0:p, u, :].rearrange("p (k a) -> p k a", a=1).to_broadcast([p, K, width])

            def enc_y(r, u, p):
                b = r * SLOTS + u
                if needed(r * 32):
                    v.wait_ge(L2["sto"][u].sem, L2["sto"][u].after(r * 32))
                v.wait_ge(L2["mm2"].sem, L2["mm2"].after(b + 1))
                nc.vector.tensor_tensor(yout[u][0:p], ps[0:p, 3072:3072 + K * H2].rearrange("p (k f) -> p k f", k=K),
                                        norm_of(u, p, H2), ALU.mult).then_inc(L2["y"].sem, 1)
            node_loop(v, enc_scale, enc_y)
            end_phase(v, VE)
            edge_vector(v, E3, src_i, dst_f)
            end_phase(v, VE)

            def dec_scale(r, u, p):
                b = r * SLOTS + u
                nc.vector.tensor_scalar(dz[0:p, u, :], dis[1][0:p, bass.ds(b * K, K)], 1.0, None, ALU.mult) \
                    .then_inc(L3["sc"].sem, 1)
                v.wait_ge(L3["sc"].sem, L3["sc"].after(b + 1))
                v.wait_ge(L3["lda"][u].sem, L3["lda"][u].after(r * 16 + 16))
                nc.vector.tensor_tensor(yin[u][0:p], yin[u][0:p], dz[0:p, u, :].rearrange("p (k a) -> p k a", a=1)
                                        .to_broadcast([p, K, H2]), ALU.mult).then_inc(L3["scal"].sem, 1)
                if needed(r * 48):
                    v.wait_ge(L3["sto"][u].sem, L3["sto"][u].after(r * 48))
                v.wait_ge(L3["d2"].sem, L3["d2"].after(b + 1))
                v.wait_ge(L3["xb"].sem, L3["xb"].after(b + 1))
                nc.vector.tensor_tensor(oa[u][0:p], ps[0:p, 0:KD].rearrange("p (k f) -> p k f", k=K), xin[u][0:p],
                                        ALU.add).then_inc(L3["x3"].sem, 1)
                v.wait_ge(L3["x3"].sem, L3["x3"].after(b + 1))
                stats(v, L3, b, u, p, oa[u], dis[1])
                nc.vector.tensor_scalar(sc2[0:p, u, :], rs[0:p, :], 1.0, None, ALU.mult)
                nc.vector.scalar_tensor_tensor(out=nb2[0:p, u, :], in0=mv[0:p, :, 0], scalar=-1.0, in1=rs[0:p, :],
                                               op0=ALU.mult, op1=ALU.mult).then_inc(L3["nb"].sem, 1)

            def dec_scores(r, u, p):
                b = r * SLOTS + u
                v.wait_ge(L3["s"].sem, L3["s"].after(b + 1))
                two = ps[0:p, SCOL:SCOL + 2 * K].rearrange("p (k a) -> p k a", a=2)
                nc.vector.tensor_copy(ob[u][0:p, :, D:D + 1], two[:, :, 0:1])
                nc.vector.tensor_copy(sdb[0:p, u, :], two[:, :, 1]).then_inc(L3["so"].sem, 1)
            node_loop(v, dec_scale, dec_scores)
            end_phase(v, VE)

            def score_ring(q, u, n):
                if not (isinstance(n, int) and n <= 0):
                    v.wait_ge(A3["sto"][u].sem, A3["sto"][u].after(n))
                nc.vector.tensor_scalar(gidx[:, u, :], src_i[:, bass.ds(q * 2, 2)], 1.0, None, ALU.mult)
                nc.vector.tensor_scalar(didx[:, u, :], dst_i[:, bass.ds(q * 2, 2)], 1.0, None, ALU.mult) \
                    .then_inc(A3["ring"].sem, 1)
            for q in range(AHEAD):
                score_ring(q, q, 0)

            def scores(r, u):
                q = r * RING + u
                if u + AHEAD < RING:
                    score_ring(q + AHEAD, u + AHEAD, r * 16)
                else:
                    score_ring(q + AHEAD, u + AHEAD - RING, r * 16 + 16)
                v.wait_ge(A3["gath"][u].sem, A3["gath"][u].after(r * 64 + 64))
                nc.vector.tensor_tensor(e_[:, bass.ds(q * 2, 2)], g[:, u, :, D], gd[:, u, :], ALU.add).then_inc(A3["e"].sem, 1)
            rounds(v, scores, RING, NPAIR)
            end_phase(v, VE)
            softmax(v)
            end_phase(v, VE)

            def alpha_ring(q, u):
                nc.vector.tensor_scalar(alr[:, u, :], alpha[:, bass.ds(q * 2, 2)], 1.0, None, ALU.mult)
            edge_vector(v, B3, src_i, dst_f, alpha_ring)
            end_phase(v, VE)

        @block.tensor
        def _(pe):
            pe.wait_ge(S0["made"].sem, S0["made"].after(5))
            pe.wait_ge(S0["ld"].sem, S0["ld"].after(16 * NLD))
            nc.tensor.transpose(ps[:, 2048:2048 + D], wn[:, :], ident[:, :])
            nc.tensor.transpose(ps[:, 2048 + D:2048 + 2 * D], wfn[:, :], ident[:, :])
            nc.tensor.matmul(ps[:, 2048 + 2 * D:2048 + 2 * D + 2], wfn[:, :], acol[:, :], start=True, stop=True)
            for n in range(2):
                def count(r, u, first=False, last=False):
                    t = r * 4 + u
                    pe.wait_ge(S0["hot"].sem, S0["hot"].after(t + 1 + n * T))
                    for j in range(2):
                        o = (2 * n + j) * 512
                        i = nc.tensor.matmul(ps[:, o:o + NC // 2], oneh_p[:, u % 2, :],
                                             oneh_c[:, u % 2, j * NC // 2:(j + 1) * NC // 2], start=first, stop=last)
                    i.then_inc(S0["mm"].sem, 1)
                for u in range(4):
                    count(0, u, first=u == 0)
                with pe.Fori(1, T // 4 - 1) as r:
                    for u in range(4):
                        count(r, u)
                for u in range(4):
                    count(T // 4 - 1, u, last=u == 3)
            end_phase(pe, PE)
            end_phase(pe, PE)
            edge_tensor(pe, E0, D, gathered(E0), g)
            end_phase(pe, PE)

            def conv0_turn(r, u, p):
                b = r * SLOTS + u
                pe.wait_ge(L0["lda"][u].sem, L0["lda"][u].after(r * 16 + 16))
                if needed(b):
                    pe.wait_ge(L0["trc"].sem, L0["trc"].after(b))
                for k in range(K):
                    i = nc.tensor.transpose(ps[:, k * P:k * P + p], ain[u][0:p, k, :], ident[0:p, 0:p])
                i.then_inc(L0["tr"].sem, 1)

            def conv0_mm(r, u, p):
                b = r * SLOTS + u
                pe.wait_ge(L0["trc"].sem, L0["trc"].after(b + 1))
                if needed(b):
                    pe.wait_ge(L0["z"].sem, L0["z"].after(b))
                for k in range(K):
                    i = nc.tensor.matmul(ps[0:p, ZC + k * P:ZC + (k + 1) * P], fT[:, k, 0:p], w0t[:, :],
                                         start=True, stop=True)
                i.then_inc(L0["mm"].sem, 1)
            node_loop(pe, conv0_turn, conv0_mm)
            end_phase(pe, PE)

            def types(pe, r, u):
                q, w = r * RING + u, u % 2
                pe.wait_ge(E1["gath"][u].sem, E1["gath"][u].after(r * 32 + 32))
                if needed(q):
                    pe.wait_ge(E1["xtc"].sem, E1["xtc"].after(q))
                for c in range(2):
                    o = 512 + c * P
                    i = nc.tensor.transpose(ps[:, o:o + P], g[:, u, c, 0:D], ident[:, :])
                i.then_inc(E1["xt"].sem, 1)
                pe.wait_ge(E1["xtc"].sem, E1["xtc"].after(q + 1))
                for c in range(2):
                    if needed((q - 1) * 2 * (R + 1) + (c + 1) * (R + 1)):
                        pe.wait_ge(E1["sel"].sem, E1["sel"].after((q - 1) * 2 * (R + 1) + (c + 1) * (R + 1)))
                    for j in range(2):
                        o = 2048 + c * 1024 + j * 512
                        i = nc.tensor.matmul(ps[:, o:o + 512], xT[:, w, c, :],
                                             w1[:, j * 4:(j + 1) * 4, :].rearrange("i r o -> i (r o)"),
                                             start=True, stop=True)
                    i.then_inc(E1["xw"].sem, 1)

            def relu_ready(pe, r, u):
                pe.wait_ge(E1["relu"].sem, E1["relu"].after(r * RING + u + 1))
            edge_tensor(pe, E1, D, relu_ready, msg, types)
            end_phase(pe, PE)
            end_phase(pe, PE)
            edge_tensor(pe, E2, D, gathered(E2), g)
            end_phase(pe, PE)

            def groups(p):
                return [(0, 4), (4, 8), (8, K)]

            def enc_turn(r, u, p):
                b = r * SLOTS + u
                pe.wait_ge(L2["scal"].sem, L2["scal"].after(b + 1))
                if needed(b):
                    pe.wait_ge(L2["trc"].sem, L2["trc"].after(b))
                for k in range(K):
                    i = nc.tensor.transpose(ps[:, k * P:k * P + p], ain[u][0:p, k, :], ident[0:p, 0:p])
                i.then_inc(L2["tr"].sem, 1)

            def enc_mm(r, u, p):
                b = r * SLOTS + u
                pe.wait_ge(L2["trc"].sem, L2["trc"].after(b + 1))
                if needed(b):
                    pe.wait_ge(L2["relu"].sem, L2["relu"].after(b))
                for lo, hi in groups(p):
                    i = nc.tensor.matmul(zc_view[:, lo:hi, 0:p], we1s[:, :], fT[:, lo:hi, 0:p], start=True, stop=True)
                i.then_inc(L2["mm"].sem, 1)
                pe.wait_ge(L2["relu"].sem, L2["relu"].after(b + 1))
                if needed(b):
                    pe.wait_ge(L2["y"].sem, L2["y"].after(b))
                for k in range(K):
                    i = nc.tensor.matmul(ps[0:p, 3072 + k * H2:3072 + (k + 1) * H2], tT[:, k, 0:p], we2s[:, :],
                                         start=True, stop=True)
                i.then_inc(L2["mm2"].sem, 1)
            node_loop(pe, enc_turn, enc_mm)
            end_phase(pe, PE)
            edge_tensor(pe, E3, H2, gathered(E3), g)
            end_phase(pe, PE)

            def dec_main(r, u, p):
                b = r * SLOTS + u
                pe.wait_ge(L3["scal"].sem, L3["scal"].after(b + 1))
                if needed(b):
                    pe.wait_ge(L3["x3"].sem, L3["x3"].after(b))
                for j in range(K // 2):
                    i = nc.tensor.transpose(ps[:, j * P:j * P + p], yin[u][0:p, 2 * j:2 * j + 2, :]
                                            .rearrange("p k f -> p (k f)"), ident[0:p, 0:p])
                i.then_inc(L3["tr"].sem, 1)
                pe.wait_ge(L3["trc"].sem, L3["trc"].after(b + 1))
                if needed(b):
                    pe.wait_ge(L3["d1c"].sem, L3["d1c"].after(b))
                for lo, hi in ((0, 2), (2, 4), (4, K // 2)):
                    for h in range(2):
                        i = nc.tensor.matmul(zc_view[:, 2 * lo + h:2 * hi + h - 1:2, 0:p], wd1s[:, h, :],
                                             tT[:, lo:hi, 0:p], start=True, stop=True)
                i.then_inc(L3["d1"].sem, 1)
                pe.wait_ge(L3["d1c"].sem, L3["d1c"].after(b + 1))
                for k in range(K):
                    i = nc.tensor.matmul(ps[0:p, k * P:(k + 1) * P], fT[:, k, 0:p], wd2s[:, :], start=True, stop=True)
                i.then_inc(L3["d2"].sem, 1)

            def dec_second(r, u, p):
                b = r * SLOTS + u
                pe.wait_ge(L3["h3"].sem, L3["h3"].after(b + 1))
                if needed(b):
                    pe.wait_ge(L3["so"].sem, L3["so"].after(b))
                for n, (lo, hi) in enumerate(HG):
                    if needed(b * len(HG) + n - 1):
                        pe.wait_ge(L3["htc"].sem, L3["htc"].after(b * len(HG) + n - 1))
                    for k in range(lo, hi):
                        o = 3072 + (n % 2) * 512 + (k - lo) * P
                        i = nc.tensor.transpose(ps[:, o:o + p], ob[u][0:p, k, 0:D], ident[0:p, 0:p])
                    i.then_inc(L3["ht"].sem, 1)
                pe.wait_ge(L3["htc"].sem, L3["htc"].after(b * len(HG) + len(HG)))
                for k in range(K):
                    i = nc.tensor.matmul(ps[0:p, SCOL + 2 * k:SCOL + 2 * k + 2], hT[:, k, 0:p], vs[:, :],
                                         start=True, stop=True)
                i.then_inc(L3["s"].sem, 1)
            node_loop(pe, dec_main, dec_second)
            end_phase(pe, PE)
            end_phase(pe, PE)
            for n, kind in enumerate(TURNS):
                pe.wait_ge(M3["ready"].sem, M3["ready"].after(n + 1))
                if kind == "row":
                    nc.tensor.transpose(ps[0:1, 0:P], col[:, n:n + 1], ident[:, :]).then_inc(M3["pe"].sem, 1)
                else:
                    nc.tensor.transpose(ps[:, 0:1], names["turned"], ident[0:1, 0:1]).then_inc(M3["pe"].sem, 1)
            end_phase(pe, PE)

            def project(pe, r, u):
                q, w = r * RING + u, u % 2
                pe.wait_ge(B3["sums"].sem, B3["sums"].after(q + 1))
                if needed(q):
                    pe.wait_ge(B3["ttc"].sem, B3["ttc"].after(q))
                for c in range(2):
                    o = 512 + c * P
                    i = nc.tensor.transpose(ps[:, o:o + P], sel[:, w, c, 0, :], ident[:, :])
                i.then_inc(B3["tt"].sem, 1)
                pe.wait_ge(B3["ttc"].sem, B3["ttc"].after(q + 1))
                for c in range(2):
                    o = 2048 + w * 512 + c * P
                    i = nc.tensor.matmul(ps[:, o:o + P], xT[:, w, c, :], wft[:, :], start=True, stop=True)
                i.then_inc(B3["fin"].sem, 1)

            def mul_ready(pe, r, u):
                pe.wait_ge(B3["mul"].sem, B3["mul"].after(r * RING + u + 1))
            edge_tensor(pe, B3, D, mul_ready, msg, None, project)
            end_phase(pe, PE)

        @block.scalar
        def _(a):
            a.wait_ge(S0["deg"].sem, S0["deg"].after(NDEG))
            for n in range(2):
                i = nc.scalar.activation(dis[n][:, :], dis[n][:, :], ACT.Sqrt)
            i.then_inc(S0["root"].sem, 1)
            end_phase(a, AC)
            ln_scalar(a, A0)
            end_phase(a, AC)
            edge_scalar(a, E0, D, tot)
            end_phase(a, AC)

            def turned(signal, b, p, out_t, n, ready, free, func=ACT.Copy, bias=0.0):
                a.wait_ge(ready.sem, ready.after(b + 1))
                if needed(b):
                    a.wait_ge(free.sem, free.after(b))
                nc.scalar.activation(out_t[:, 0:n, 0:p], ps[:, 0:n * P].rearrange("f (k p) -> f k p", p=P)[:, :, 0:p],
                                     func, bias=bias).then_inc(signal.sem, 1)

            def conv0_first(r, u, p):
                b = r * SLOTS + u
                turned(L0["trc"], b, p, fT, K, L0["tr"], L0["mm"])
                a.wait_ge(L0["sc"].sem, L0["sc"].after(b + 1))
                a.wait_ge(L0["ld"][u].sem, L0["ld"][u].after(r * 16 + 16))
                if needed(b - SLOTS + 1):
                    a.wait_ge(L0["res"].sem, L0["res"].after(b - SLOTS + 1))
                relu_rows(a, p, ob_h[u], xin[u], sc[:, u, :], nbi[:, u, :]).then_inc(L0["h"].sem, 1)

            def conv0_second(r, u, p):
                b = r * SLOTS + u
                root(a, L0, b, p)
                a.wait_ge(L0["nb"].sem, L0["nb"].after(b * 2 + 2))
                if needed(r * 32):
                    a.wait_ge(L0["sto"][u].sem, L0["sto"][u].after(r * 32))
                relu_rows(a, p, hb[u], oa[u], sc2[:, u, :], nb2[:, u, :]).then_inc(L0["h1"].sem, 1)
            node_loop(a, conv0_first, conv0_second)
            end_phase(a, AC)

            def rows_turned(r, u):
                q, w = r * RING + u, u % 2
                if needed((q - 1) * 2):
                    a.wait_ge(E1["xw"].sem, E1["xw"].after((q - 1) * 2))
                a.wait_ge(E1["xt"].sem, E1["xt"].after(q + 1))
                nc.scalar.activation(xT[:, w, :, :], ps[:, 512:512 + 2 * P]
                                     .rearrange("p (c f) -> p c f", c=2), ACT.Copy).then_inc(E1["xtc"].sem, 1)
            rows_turned(0, 0)

            def e1_body(r, u):
                q, w = r * RING + u, u % 2
                r1, u1 = (r, u + 1) if u + 1 < RING else (r + 1, 0)
                rows_turned(r1, u1)
                if needed(q - 1):
                    a.wait_ge(E1["mm"].sem, E1["mm"].after(q - 1))
                a.wait_ge(E1["sel"].sem, E1["sel"].after((q + 1) * 2 * (R + 1)))
                nc.scalar.activation(msg[:, w, :, :], sel[:, w, :, 0, :], ACT.Relu).then_inc(E1["relu"].sem, 1)
                if needed((q - RING + 1) * 32):
                    a.wait_ge(E1["scat"].sem, E1["scat"].after((q - RING + 1) * 32))
                a.wait_ge(E1["mm"].sem, E1["mm"].after(q + 1))
                nc.scalar.activation(tot[:, u, :, :], pair_sums(w, D), ACT.Copy).then_inc(E1["tot"].sem, 1)
            rounds(a, e1_body, RING, NPAIR)
            end_phase(a, AC)
            ln_scalar(a, A2)
            end_phase(a, AC)
            edge_scalar(a, E2, D, tot)
            end_phase(a, AC)

            def enc_first(r, u, p):
                turned(L2["trc"], r * SLOTS + u, p, fT, K, L2["tr"], L2["mm"])

            def enc_second(r, u, p):
                b = r * SLOTS + u
                a.wait_ge(L2["mm"].sem, L2["mm"].after(b + 1))
                if needed(b):
                    a.wait_ge(L2["mm2"].sem, L2["mm2"].after(b))
                nc.scalar.activation(tT[:, :, 0:p], zc_view[:, :, 0:p], ACT.Relu, bias=be1c[:, :]).then_inc(L2["relu"].sem, 1)
            node_loop(a, enc_first, enc_second)
            end_phase(a, AC)
            edge_scalar(a, E3, H2, toty)
            end_phase(a, AC)

            def dec_first(r, u, p):
                b = r * SLOTS + u
                turned(L3["trc"], b, p, tT, K // 2, L3["tr"], L3["d1"], ACT.Relu, be2c[:, :])
                a.wait_ge(L3["d1"].sem, L3["d1"].after(b + 1))
                if needed(b):
                    a.wait_ge(L3["d2"].sem, L3["d2"].after(b))
                nc.scalar.activation(fT[:, :, 0:p], zc_view[:, :, 0:p], ACT.Relu, bias=bd1c[:, :]).then_inc(L3["d1c"].sem, 1)
                root(a, L3, b, p)

            def dec_h3(r, u, p):
                b = r * SLOTS + u
                a.wait_ge(L3["nb"].sem, L3["nb"].after(b + 1))
                if needed(r * 48):
                    a.wait_ge(L3["sto"][u].sem, L3["sto"][u].after(r * 48))
                relu_rows(a, p, ob[u], oa[u], sc2[:, u, :], nb2[:, u, :]).then_inc(L3["h3"].sem, 1)
                for n, (lo, hi) in enumerate(HG):
                    a.wait_ge(L3["ht"].sem, L3["ht"].after(b * len(HG) + n + 1))
                    if n == 0:
                        if needed(b):
                            a.wait_ge(L3["s"].sem, L3["s"].after(b))
                    nc.scalar.activation(hT[:, lo:hi, 0:p], ps[:, 3072 + (n % 2) * 512:3072 + (n % 2) * 512 + (hi - lo) * P]
                                         .rearrange("f (k p) -> f k p", p=P)[:, :, 0:p], ACT.Copy).then_inc(L3["htc"].sem, 1)
            node_loop(a, dec_first, dec_h3)
            end_phase(a, AC)
            end_phase(a, AC)
            a.wait_ge(M3["diff"].sem, M3["diff"].after(1))
            nc.scalar.activation(wgt[:, :], wgt[:, :], ACT.Exp).then_inc(M3["exp"].sem, 1)
            end_phase(a, AC)

            def weigh(r, u):
                q, w = r * RING + u, u % 2
                a.wait_ge(B3["ring"].sem, B3["ring"].after(q + 1))
                if needed(q - 1):
                    a.wait_ge(B3["mm"].sem, B3["mm"].after(q - 1))
                a.wait_ge(B3["load"][u].sem, B3["load"][u].after(r * 32 + 32))
                for c in range(2):
                    i = nc.scalar.activation(msg[:, w, c, :], g[:, u, c, 0:D], ACT.Copy, scale=alr[:, u, c:c + 1])
                i.then_inc(B3["mul"].sem, 1)

            def b3_body(r, u):
                q, w = r * RING + u, u % 2
                weigh(r, u)
                a.wait_ge(B3["mm"].sem, B3["mm"].after(q + 1))
                if needed(q - 1):
                    a.wait_ge(B3["tt"].sem, B3["tt"].after(q - 1))
                nc.scalar.activation(sel[:, w, :, 0, :], pair_sums(w, D), ACT.Copy).then_inc(B3["sums"].sem, 1)
                a.wait_ge(B3["tt"].sem, B3["tt"].after(q + 1))
                if needed(q - 1):
                    a.wait_ge(B3["fin"].sem, B3["fin"].after(q - 1))
                nc.scalar.activation(xT[:, w, :, :], ps[:, 512:512 + 2 * P]
                                     .rearrange("p (c f) -> p c f", c=2), ACT.Copy).then_inc(B3["ttc"].sem, 1)
                a.wait_ge(B3["fin"].sem, B3["fin"].after(q + 1))
                if needed((q - RING + 1) * 32):
                    a.wait_ge(B3["scat"].sem, B3["scat"].after((q - RING + 1) * 32))
                nc.scalar.activation(tot[:, u, :, :], ps[:, 2048 + w * 512:2048 + w * 512 + 256]
                                     .rearrange("p (c f) -> p c f", c=2), ACT.Copy).then_inc(B3["tot"].sem, 1)
            rounds(a, b3_body, RING, NPAIR)
            end_phase(a, AC)


_INS = ["x", "src", "dst", "edge_attr_32", "edge_type_8", "L0_gnn_W", "L0_gnn_b", "L1_gnn_weight", "L1_gnn_bias",
        "L2_gnn_W_enc1", "L2_gnn_b_enc1", "L2_gnn_W_enc2", "L2_gnn_b_enc2", "L2_gnn_W_dec1", "L2_gnn_b_dec1",
        "L2_gnn_W_dec2", "L2_gnn_b_dec2", "L3_gnn_W_fc", "L3_gnn_W_attn"]


def kernel(**inputs):
    import numpy as _np
    import concourse.bacc as _bacc
    from concourse import mybir as _mybir
    from concourse.bass_utils import run_bass_kernel_spmd as _run

    nc = _bacc.Bacc("TRN2", target_bir_lowering=False, num_devices=1)
    arrays, args = {}, []
    for name in _INS:
        a = _np.ascontiguousarray(inputs[name])
        arrays[f"in_{name}"] = a
        args.append(nc.dram_tensor(f"in_{name}", a.shape, _mybir.dt.from_np(a.dtype), kind="ExternalInput").ap())
    args.append(nc.dram_tensor("out_rows", (NR, D), _mybir.dt.float32, kind="ExternalOutput").ap())
    gnn(nc, *args)
    r = _run(nc, [arrays], core_ids=[0])
    return r.results[0]["out_rows"][:N]
```

```python
import concourse.bass as bass
from concourse import mybir
from contextlib import ExitStack

F32 = mybir.dt.float32
F16 = mybir.dt.float16
I32 = mybir.dt.int32
ALU = mybir.AluOpType
ACT = mybir.ActivationFunctionType
AX = mybir.AxisListType

N, E, D, H2, DE, R = 100000, 50000, 128, 64, 32, 8
P = 128
EPS = 1e-5
BIG = 1e30
ROUND = 1.5 * 2 ** 23

K = 10
BR = P * K
NB = N // BR
PT = (N - NB * BR) // K
NC = (NB + 1) * K
SLOTS = 3
assert NB % SLOTS == 0 and PT * K + NB * BR == N

T = 392
LASTP = E // T
LASTN = E - LASTP * T
NPAIR = T // 2
RING = 7
UNROLL = 2 * RING
AHEAD = 4
SCORE_AHEAD = 3
TX = T + 2 * AHEAD
NR = N + 2 * P
EXTRA = {"ring": AHEAD, "kt": 1, "tx": 2, "txc": 2, "masked": 1, "xw": 1, "bn": 1, "mv": 1, "var": 1}
assert LASTP == P - 1 and NPAIR % UNROLL == 0 and NPAIR > UNROLL


def needed(count):
    return not isinstance(count, int) or count > 0


class Count:
    def __init__(self, sem, base):
        self.sem, self.base = sem, base

    def after(self, n):
        return self.base + n


def node_loop(eng, *stages):
    most = max(lag for _, lag in stages)
    peeled = (SLOTS + most + SLOTS - 1) // SLOTS

    def at(b):
        for fn, lag in stages:
            if 0 <= b - lag <= NB:
                fn((b - lag) // SLOTS, (b - lag) % SLOTS, PT if b - lag == NB else P)
    for b in range(peeled * SLOTS):
        at(b)
    with eng.Fori(peeled, NB // SLOTS) as r:
        for u in range(SLOTS):
            for fn, lag in stages:
                back = (lag - u + SLOTS - 1) // SLOTS if lag > u else 0
                fn(r - back if back else r, u - lag + back * SLOTS, P)
    for b in range(NB, NB + 1 + most):
        at(b)


class Pair:
    def __init__(self, r, u):
        while u >= UNROLL:
            r, u = r + 1, u - UNROLL
        while u < 0:
            r, u = r - 1, u + UNROLL
        self.r, self.u = r, u
        self.q = r * UNROLL + u
        self.n = r * (UNROLL // RING) + u // RING
        self.k, self.w = u % RING, u % 2

    def plus(self, d):
        return Pair(self.r, self.u + d)


def pair_loop(eng, *stages):
    def at(q):
        for fn, lag in stages:
            if 0 <= q - lag < NPAIR:
                fn(Pair(0, q - lag) if q - lag < UNROLL else Pair((q - lag) // UNROLL, (q - lag) % UNROLL))
    for q in range(UNROLL):
        at(q)
    with eng.Fori(1, NPAIR // UNROLL) as r:
        for u in range(UNROLL):
            for fn, lag in stages:
                fn(Pair(r, u).plus(-lag) if lag else Pair(r, u))
    for q in range(NPAIR, NPAIR + max(lag for _, lag in stages)):
        at(q)


def gnn(nc, x, src, dst, ea, et, w_l0, b_l0, w_l1, b_l1, we1, be1, we2, be2, wd1, bd1, wd2, bd2,
        w_fc, w_at, out):
    with ExitStack() as ctx:
        def sb(name, shape, dt=F32):
            return ctx.enter_context(nc.sbuf_tensor(name, shape, dt))

        def dram(name, shape):
            return nc.dram_tensor(name, shape, F32, kind="Internal").ap()

        made = {}

        def phase(family, per, counts, slotted=None):
            def count(name, total):
                sem, base = made.get(f"{family}_{name}") or (ctx.enter_context(nc.semaphore(f"{family}_{name}")), 0)
                made[f"{family}_{name}"] = sem, base + total
                return Count(sem, base)
            names = {}
            for n in counts.split():
                name, _, times = n.partition(":")
                names[name] = count(name, per * int(times or 1) + EXTRA.get(name, 0) * (family == "edge"))
            for name, totals in (slotted or {}).items():
                names[name] = [count(f"{name}{i}", n) for i, n in enumerate(totals)]
            return names

        t_src = dram("t_src", (N, D))
        t_h1 = dram("t_h1", (N, D + 1))
        t_acc = dram("t_acc", (NR, D))
        t_x = dram("t_x", (NR, D))
        t_y = dram("t_y", (N, H2))
        t_yacc = dram("t_yacc", (NR, H2))
        t_z = dram("t_z", (T, P, D))

        ps = ctx.enter_context(nc.psum_tensor("ps", [P, 4096], F32))

        ident = sb("ident", [P, P])
        ones = sb("ones", [P, P])
        ioc = sb("ioc", [P, NC], F16)
        iop = sb("iop", [P, P], F16)
        earlier = sb("earlier", [P, 2, 2 * P])
        spare = sb("spare", [P, 2])
        zero = sb("zero", [P, 2 * D])
        w0t = sb("w0t", [D, D])
        wn = sb("wn", [D, D])
        w1 = sb("w1", [D, R, D])
        we1s = sb("we1s", [D, D])
        we2s = sb("we2s", [D, H2])
        wd1s = sb("wd1s", [P, 2, D])
        wd2s = sb("wd2s", [D, D])
        wfn = sb("wfn", [D, D])
        wft = sb("wft", [D, D])
        acol = sb("acol", [D, 1])
        asb = sb("asb", [P, D])
        vdb = sb("vdb", [P, D])
        b0b = sb("b0b", [P, D])
        b1b = sb("b1b", [P, D])
        bd2b = sb("bd2b", [P, D])
        aeb = sb("aeb", [P, DE])
        be1c = sb("be1c", [D, 1])
        be2c = sb("be2c", [2 * H2, 1])
        bd1c = sb("bd1c", [D, 1])

        src_i = sb("src_i", [P, TX], I32)
        dst_i = sb("dst_i", [P, TX], I32)
        typ_i = sb("typ_i", [P, TX], I32)
        src_f = sb("src_f", [P, TX])
        dst_f = sb("dst_f", [P, TX])
        typ_f = sb("typ_f", [P, TX])
        hcol = [sb(f"hcol{i}", [P, T]) for i in range(2)]
        hpar = [sb(f"hpar{i}", [P, T]) for i in range(2)]
        ta = sb("ta", [P, T])
        tb = sb("tb", [P, T])
        tcv = sb("tcv", [P, T])
        dis = [sb("dis_src", [P, NC]), sb("dis_dst", [P, NC])]
        mean_r = sb("mean_r", [P, NC])
        rstd_r = sb("rstd_r", [P, NC])

        gidx = sb("gidx", [P, RING, 2], I32)
        didx = sb("didx", [P, RING, 2], I32)
        sidx = sb("sidx", [P, RING, 2], I32)
        keyr = sb("keyr", [P, RING, 2])
        keyd = sb("keyd", [P, RING, 2])
        typr = sb("typr", [P, RING, 2])
        alr = sb("alr", [P, RING, 2])
        cnt = sb("cnt", [P, 2, 2])
        mdup = sb("mdup", [P, 2, 2])
        seq = sb("seq", [P, 2, 2, 2 * P])
        junk = sb("junk", [P, 2, 2 * P])
        g = sb("g", [P, RING, 2, D])
        sco = sb("sco", [P, 2, 2, 2])
        est = sb("est", [P, 2, 4, 6])
        emv = sb("emv", [P, 2, 4, 2])
        evar = sb("evar", [P, 2, 4])
        estd = sb("estd", [P, 2, 4])
        ers = sb("ers", [P, 2, 4])
        esc = sb("esc", [P, 2, 4])
        enb = sb("enb", [P, 2, 4])
        tot = sb("tot", [P, RING, 2, D])
        msg = sb("msg", [P, 2, 2, D])
        toty = sb("toty", [P, RING, 2, H2])
        gy = sb("gy", [P, RING, 2, H2])
        xT = sb("xT", [P, 2, 2 * 2 * P])
        oneh_p = sb("oneh_p", [P, 4, P], F16)
        oneh_c = sb("oneh_c", [P, 4, NC], F16)
        zero16 = sb("zero16", [P, P], F16)

        KD = K * D
        dense = sb("dense", [P, 15 * KD])

        def area(n):
            return dense[:, n * KD:(n + 1) * KD].rearrange("p (k f) -> p k f", k=K)
        xin = [area(i) for i in range(3)]
        ain = [area(3 + i) for i in range(3)]
        oa = [area(6 + i) for i in range(3)]
        yin = [dense[:, (3 + i) * KD:(3 + i) * KD + K * H2].rearrange("p (k f) -> p k f", k=K) for i in range(3)]
        yout = [dense[:, (6 + i) * KD:(6 + i) * KD + K * H2].rearrange("p (k f) -> p k f", k=K) for i in range(3)]
        hb = [sb(f"hb{i}", [P, K, D + 1]) for i in range(3)]
        tT = [area(12 + i) for i in range(3)]
        fT = [sb(f"fT{i}", [P, K, P]) for i in range(3)]
        ob_h = tT
        dz = sb("dz", [P, SLOTS, K])
        col2 = sb("col2", [P, 4])
        CNT = 4 * 512
        XW = 5 * 512
        TURN = (1 * 512, 4 * 512)
        SUMS = 2 * 512
        ZC = 3 * 512
        zc_view = ps[:, ZC:ZC + KD].rearrange("f (k p) -> f k p", k=K)
        NLD = 18
        NDEG = 20
        HC = 2 * 512
        DC = 5 * 512
        hid_view = ps[:, HC:HC + KD].rearrange("f (k p) -> f k p", k=K)
        dec_view = ps[:, DC:DC + KD].rearrange("p (k f) -> p k f", k=K)
        row = dense[0:1, 13 * KD:13 * KD + 13 * P].rearrange("p (n f) -> p n f", n=13)
        TURNS = "row row row col row row col row col row row col".split()
        names = {n: row[0:1, j, :] for j, n in enumerate(
            ("first", "last", "contp", "contn", "single", "t", "neg", "scan", "cinn", "dn", "base", "turn", "turned"))}
        st = sb("st", [P, K, 6])
        mv = sb("mv", [P, K, 2])
        var = sb("var", [P, K])
        std = sb("std", [P, K])
        rs = sb("rs", [P, K])
        sc = sb("sc", [P, SLOTS, K])
        nbi = sb("nbi", [P, SLOTS, K])
        sc2 = sb("sc2", [P, SLOTS, K])
        nb2 = sb("nb2", [P, SLOTS, K])
        dsl = sb("dsl", [P, SLOTS, K])
        nsrc = sb("nsrc", [P, TX])
        enorm = sb("enorm", [P, 2, 2])
        EH = T // 4
        eas = [dense[:, i * EH * DE:(i + 1) * EH * DE].rearrange("p (t d) -> p t d", d=DE) for i in range(2)]
        prod = dense[:, 2 * EH * DE:3 * EH * DE].rearrange("p (t d) -> p t d", d=DE)
        xm = dense[:, 0:2 * R * 2 * P].rearrange("p (w r e) -> p w r e", w=2, r=R)
        gn = dense[:, 2 * R * 2 * P:2 * R * 2 * P + RING * 2 * (D + 1)].rearrange("p (k c f) -> p k c f", k=RING, c=2)
        gd = dense[:, 0:RING * 2 * D].rearrange("p (k c f) -> p k c f", k=RING, c=2)
        zrow = area(8)
        scans = [dense[:, 9 * KD + i * TX:9 * KD + (i + 1) * TX] for i in range(10)]
        e_, alpha = scans[0:2]
        se, fwd, bwd, same, nsame, gsame, gnot, wgt = (t[:, 0:T] for t in scans[2:])
        col = sb("col", [P, 12])

        gate = ctx.enter_context(nc.semaphore("phase_done"))
        tick = ctx.enter_context(nc.semaphore("pool_tick"))
        phases = [0, 0, 0, 0, 0]
        block = ctx.enter_context(nc.Block())

        def end_phase(eng, who):
            phases[who] += 1
            eng.drain().then_inc(gate, 1)
            eng.wait_ge(gate, 5 * phases[who])

        SP, AC, VE, PE, PO = range(5)

        def rows_of(table, b, p):
            return table[bass.ds(b * BR, p * K), :].rearrange("(p k) f -> p k f", k=K)

        def slots(n):
            return [n * len(range(u, NB + 1, SLOTS)) for u in range(SLOTS)]

        S0 = phase("setup", 1, "ld lde zero pad made calc deg hot mm root")
        LN = "copy bn mv var std rs sc "
        A0 = phase("node", NB + 1, LN + "nb h", {"ld": slots(16), "sto": slots(32)})
        EN = "ring kt s cnt mdup sidx mm tot scat:32 "
        GA = {"gath": [32 * len(range(k, NPAIR + AHEAD, RING)) for k in range(RING)]}
        E0 = phase("edge", NPAIR, EN + "hot count", GA)
        C0 = phase("target_degrees", 1, "v close root")
        L0 = phase("node", NB + 1, LN + "nb dz h tr trc mm z xh res h1",
                   {"ld": slots(16), "lda": slots(16), "sto": slots(32)})
        E1 = phase("edge", NPAIR, EN + "tx txc masked xw relu zrow zeroed", GA)
        E2 = phase("edge", NPAIR, EN + "bn mv var std rs sc nb h", GA)
        L2 = phase("node", NB + 1, LN + "nb h add dz scal tr trc mm relu mm2 y",
                   {"ld": slots(16), "lda": slots(16), "sto": slots(32)})
        E3 = phase("edge", NPAIR, EN, GA)
        L3 = phase("node", NB + 1, "sc scal tr trc d1 d1c d2 xb x3",
                   {"ld": slots(16), "lda": slots(16), "sto": slots(16)})
        A3 = phase("node", NPAIR, "ring bn mv var std rs nb h tr trc mm z dot e", {"gath": [0] * RING, "sto": [0] * RING})
        M3 = phase("softmax", 1, "v ready pe ex diff exp", {"ld": [0] * 4})
        B3 = phase("edge", NPAIR, EN + "mul", {"load": [0] * RING})

        def edge_pool(gp, s, table, target, t_out, rows=None):
            def gath(p):
                gp.wait_ge(s["ring"].sem, s["ring"].after(p.q + 1))
                gp.sem_inc(tick, 1)
                for c in range(2):
                    gp.indirect_dma_start(rows[:, p.k, c, :], None, table,
                                          bass.IndirectOffsetOnAxis(ap=gidx[:, p.k, c:c + 1], axis=0)) \
                        .then_inc(s["gath"][p.k].sem, 16)
            if table is not None:
                for q in range(AHEAD):
                    gath(Pair(0, q))

            def body(p):
                if table is not None:
                    gath(p.plus(AHEAD))
                gp.wait_ge(s["sidx"].sem, s["sidx"].after(p.q + 1))
                gp.sem_inc(tick, 1)
                gp.wait_ge(s["tot"].sem, s["tot"].after(p.q + 1))
                gp.sem_inc(tick, 1)
                if needed(p.q):
                    gp.wait_ge(s["scat"].sem, s["scat"].after(p.q * 32))
                    gp.sem_inc(tick, 1)
                for c in range(2):
                    gp.indirect_dma_start(target, bass.IndirectOffsetOnAxis(ap=sidx[:, p.k, c:c + 1], axis=0),
                                          t_out[:, p.k, c, :], None, compute_op=ALU.add).then_inc(s["scat"].sem, 16)
            pair_loop(gp, (body, 0))
            if table is not None:
                for q in range(NPAIR, NPAIR + AHEAD):
                    gp.wait_ge(s["gath"][q % RING].sem, s["gath"][q % RING].after(32 * (q // RING + 1)))
            gp.wait_ge(s["scat"].sem, s["scat"].after(32 * NPAIR))

        def edge_vector(v, s, gi, key, more=None, early=None, between=None):
            def ring(p):
                if needed(p.q - RING + 1):
                    v.wait_ge(s["scat"].sem, s["scat"].after((p.q - RING + 1) * 32))
                nc.vector.tensor_scalar(gidx[:, p.k, :], gi[:, bass.ds(p.q * 2, 2)], 1.0, None, ALU.mult)
                if more is not None:
                    more(p)
                nc.vector.tensor_scalar(keyr[:, p.k, :], key[:, bass.ds(p.q * 2, 2)], 1.0, None, ALU.mult) \
                    .then_inc(s["ring"].sem, 1)
            for q in range(AHEAD):
                ring(Pair(0, q))
            if early is not None:
                early(Pair(0, 0))

            def body(p):
                ring(p.plus(AHEAD))
                v.wait_ge(s["kt"].sem, s["kt"].after(p.q + 1))
                if needed(p.q - 1):
                    v.wait_ge(s["mm"].sem, s["mm"].after(p.q - 1))
                for c in range(2):
                    i = nc.vector.tensor_scalar(seq[:, p.w, c, :], ps[:, 0:2 * P], keyr[:, p.k, c:c + 1],
                                                None, ALU.is_equal)
                i.then_inc(s["s"].sem, 1)
                if early is not None:
                    early(p.plus(1))
                if between is not None:
                    between(p)
                v.wait_ge(s["s"].sem, s["s"].after(p.q + 1))
                nc.vector.tensor_tensor(keyd[:, p.k, :], spare[:, :], keyr[:, p.k, :], ALU.subtract)
                for c in range(2):
                    i = nc.vector.tensor_tensor_reduce(out=junk[:, c, :], in0=seq[:, p.w, c, :], in1=earlier[:, c, :],
                                                       scale=1.0, scalar=0.0, op0=ALU.mult, op1=ALU.add,
                                                       accum_out=cnt[:, p.w, c:c + 1])
                i.then_inc(s["cnt"].sem, 1)
                v.wait_ge(s["cnt"].sem, s["cnt"].after(p.q + 1))
                nc.vector.scalar_tensor_tensor(out=mdup[:, p.w, :], in0=cnt[:, p.w, :], scalar=1.0, in1=keyd[:, p.k, :],
                                               op0=ALU.min, op1=ALU.mult).then_inc(s["mdup"].sem, 1)
                v.wait_ge(s["mdup"].sem, s["mdup"].after(p.q + 1))
                nc.vector.tensor_tensor(sidx[:, p.k, :], mdup[:, p.w, :], keyr[:, p.k, :], ALU.add) \
                    .then_inc(s["sidx"].sem, 1)
            pair_loop(v, (body, 0))

        def edge_tensor(pe, s, width, ready, rows, ring, prologue=None, ahead=None, between=None, after=None):
            def keys(p):
                pe.wait_ge(s["ring"].sem, s["ring"].after(p.q + 1))
                if needed(p.q):
                    pe.wait_ge(s["s"].sem, s["s"].after(p.q))
                for c in range(2):
                    i = nc.tensor.transpose(ps[:, c * P:(c + 1) * P], keyr[:, p.k, c:c + 1].to_broadcast([P, P]),
                                            ident[:, :])
                i.then_inc(s["kt"].sem, 1)
            keys(Pair(0, 0))
            if prologue is not None:
                prologue()

            def body(p):
                if ahead is not None:
                    ahead(p)
                keys(p.plus(1))
                if between is not None:
                    between(p)
                pe.wait_ge(s["s"].sem, s["s"].after(p.q + 1))
                ready(p)
                if needed(p.q - 1):
                    pe.wait_ge(s["tot"].sem, s["tot"].after(p.q - 1))
                for d in range(2):
                    o = SUMS + p.w * 512 + d * P
                    for c in range(2):
                        i = nc.tensor.matmul(ps[:, o:o + width], seq[:, p.w, c, d * P:(d + 1) * P],
                                             rows[:, p.k if ring == RING else p.w, c, :], start=(c == 0), stop=(c == 1))
                i.then_inc(s["mm"].sem, 1)
                if after is not None:
                    after(p)
            pair_loop(pe, (body, 0))

        def gathered(pe, s):
            def ready(p):
                pe.wait_ge(s["gath"][p.k].sem, s["gath"][p.k].after(p.n * 32 + 32))
            return ready

        def pair_of(o, width=D):
            return ps[:, o:o + 2 * P].rearrange("p (c f) -> p c f", c=2)[:, :, 0:width]

        def sums_out(a, s, p, t_out, width):
            if needed(p.q - RING + 1):
                a.wait_ge(s["scat"].sem, s["scat"].after((p.q - RING + 1) * 32))
            a.wait_ge(s["mm"].sem, s["mm"].after(p.q + 1))
            nc.scalar.activation(t_out[:, p.k, :, :], pair_of(SUMS + p.w * 512, width), ACT.Copy) \
                .then_inc(s["tot"].sem, 1)

        def edge_stats(v, s, p, tiles, meanwhile):
            if needed(p.q - 1):
                v.wait_ge(s["nb"].sem, s["nb"].after(p.q - 1))
            for j, t in enumerate(tiles):
                i = nc.vector.bn_stats(est[:, p.w, j, :], t)
            i.then_inc(s["bn"].sem, 1)
            v.wait_ge(s["bn"].sem, s["bn"].after(p.q + 1))
            meanwhile(p)
            for j in range(len(tiles)):
                i = nc.vector.bn_aggr(emv[:, p.w, j, :], est[:, p.w, j, :])
            i.then_inc(s["mv"].sem, 1)
            v.wait_ge(s["mv"].sem, s["mv"].after(p.q + 1))
            nc.vector.tensor_scalar(evar[:, p.w, 0:len(tiles)], emv[:, p.w, 0:len(tiles), 1], EPS, None, ALU.add) \
                .then_inc(s["var"].sem, 1)

        def edge_scales(v, s, p, n):
            v.wait_ge(s["std"].sem, s["std"].after(p.q + 1))
            if needed(p.q - 1):
                v.wait_ge(s["h"].sem, s["h"].after(p.q - 1))
            nc.vector.reciprocal(ers[:, p.w, 0:n], estd[:, p.w, 0:n]).then_inc(s["rs"].sem, 1)
            v.wait_ge(s["rs"].sem, s["rs"].after(p.q + 1))

        def edge_bias(s, p, n, scale):
            nc.vector.scalar_tensor_tensor(out=enb[:, p.w, 0:n], in0=emv[:, p.w, 0:n, 0], scalar=-1.0,
                                           in1=scale[:, p.w, 0:n], op0=ALU.mult, op1=ALU.mult).then_inc(s["nb"].sem, 1)

        def edge_root(a, s, p, n):
            a.wait_ge(s["var"].sem, s["var"].after(p.q + 1))
            nc.scalar.activation(estd[:, p.w, 0:n], evar[:, p.w, 0:n], ACT.Sqrt).then_inc(s["std"].sem, 1)

        def edge_relu(a, s, p, pairs, scale):
            a.wait_ge(s["nb"].sem, s["nb"].after(p.q + 1))
            for j, (o, t) in enumerate(pairs):
                i = nc.scalar.activation(o, t, ACT.Relu, bias=enb[:, p.w, j:j + 1], scale=scale[:, p.w, j:j + 1])
            i.then_inc(s["h"].sem, 1)

        def stats(v, s, b, u, p, xt, d_src):
            for k in range(K):
                i = nc.vector.bn_stats(st[0:p, k, :], xt[0:p, k, :])
            i.then_inc(s["bn"].sem, 1)
            v.wait_ge(s["bn"].sem, s["bn"].after(b + 1))
            nc.vector.tensor_scalar(dsl[0:p, u, :], d_src[0:p, bass.ds(b * K, K)], 1.0, None, ALU.mult) \
                .then_inc(s["copy"].sem, 1)
            for k in range(K):
                i = nc.vector.bn_aggr(mv[0:p, k, :], st[0:p, k, :])
            i.then_inc(s["mv"].sem, 1)
            v.wait_ge(s["mv"].sem, s["mv"].after(b + 1))
            nc.vector.tensor_scalar(var[0:p, :], mv[0:p, :, 1], EPS, None, ALU.add).then_inc(s["var"].sem, 1)

        def rstd(v, s, b, p):
            v.wait_ge(s["std"].sem, s["std"].after(b + 1))
            nc.vector.reciprocal(rs[0:p, :], std[0:p, :]).then_inc(s["rs"].sem, 1)
            v.wait_ge(s["rs"].sem, s["rs"].after(b + 1))

        def row_scales(v, s):
            def body(r, u, p):
                rstd(v, s, r * SLOTS + u, p)
                nc.vector.tensor_scalar(sc2[0:p, u, :], rs[0:p, :], 1.0, None, ALU.mult)
                nc.vector.scalar_tensor_tensor(out=nb2[0:p, u, :], in0=mv[0:p, :, 0], scalar=-1.0, in1=rs[0:p, :],
                                               op0=ALU.mult, op1=ALU.mult).then_inc(s["nb"].sem, 1)
            return body

        def root(a, s, b, p):
            a.wait_ge(s["var"].sem, s["var"].after(b + 1))
            nc.scalar.activation(std[0:p, :], var[0:p, :], ACT.Sqrt).then_inc(s["std"].sem, 1)

        def relu_rows(a, p, out_t, in_t, scale, bias):
            for k in range(K):
                i = nc.scalar.activation(out_t[0:p, k, 0:D], in_t[0:p, k, :], ACT.Relu, bias=bias[0:p, k:k + 1],
                                         scale=scale[0:p, k:k + 1])
            return i

        def ln_sync(sp, s, table):
            def load(r, u, p):
                b = r * SLOTS + u
                if needed(b - SLOTS + 1):
                    sp.wait_ge(s["h"].sem, s["h"].after(b - SLOTS + 1))
                sp.dma_start(xin[u][0:p], rows_of(table, b, p)).then_inc(s["ld"][u].sem, 16)

            def store(r, u, p):
                b = r * SLOTS + u
                sp.wait_ge(s["h"].sem, s["h"].after(b + 1))
                sp.dma_start(rows_of(t_src, b, p), oa[u][0:p]).then_inc(s["sto"][u].sem, 16)
                sp.dma_start(rows_of(t_acc, b, p), oa[u][0:p]).then_inc(s["sto"][u].sem, 16)
            node_loop(sp, (load, 0), (store, 2))
            stored(sp, s, 32)

        def stored(sp, s, per):
            for u in range(SLOTS):
                sp.wait_ge(s["sto"][u].sem, s["sto"][u].after(per * len(range(u, NB + 1, SLOTS))))

        def ln_vector(v, s, d_src):
            def body(r, u, p):
                b = r * SLOTS + u
                v.wait_ge(s["ld"][u].sem, s["ld"][u].after(r * 16 + 16))
                stats(v, s, b, u, p, xin[u], d_src)
                rstd(v, s, b, p)
                nc.vector.tensor_tensor(sc[0:p, u, :], rs[0:p, :], dsl[0:p, u, :], ALU.mult).then_inc(s["sc"].sem, 1)
                nc.vector.tensor_scalar(rstd_r[0:p, bass.ds(b * K, K)], rs[0:p, :], 1.0, None, ALU.mult)
                nc.vector.scalar_tensor_tensor(out=mean_r[0:p, bass.ds(b * K, K)], in0=mv[0:p, :, 0], scalar=-1.0,
                                               in1=rs[0:p, :], op0=ALU.mult, op1=ALU.mult)
                v.wait_ge(s["sc"].sem, s["sc"].after(b + 1))
                nc.vector.scalar_tensor_tensor(out=nbi[0:p, u, :], in0=mv[0:p, :, 0], scalar=-1.0, in1=sc[0:p, u, :],
                                               op0=ALU.mult, op1=ALU.mult).then_inc(s["nb"].sem, 1)
            node_loop(v, (body, 0))

        def ln_scalar(a, s):
            def body(r, u, p):
                b = r * SLOTS + u
                root(a, s, b, p)
                if needed(r * 32):
                    a.wait_ge(s["sto"][u].sem, s["sto"][u].after(r * 32))
                a.wait_ge(s["nb"].sem, s["nb"].after(b + 1))
                relu_rows(a, p, oa[u], xin[u], sc[:, u, :], nbi[:, u, :]).then_inc(s["h"].sem, 1)
            node_loop(a, (body, 0))

        @block.sync
        def _(sp):
            sp.dma_start(wn[:, :], w_l0).then_inc(S0["ld"].sem, 16)
            sp.dma_start(w1[:, :, :], w_l1.rearrange("r i o -> i r o")).then_inc(S0["ld"].sem, 16)
            sp.dma_start(we1s[:, :], we1).then_inc(S0["ld"].sem, 16)
            sp.dma_start(we2s[:, :], we2).then_inc(S0["ld"].sem, 16)
            for h in range(2):
                sp.dma_start(be2c[h * H2:(h + 1) * H2, :], be2.rearrange("(p a) -> p a", a=1)).then_inc(S0["ld"].sem, 16)
            sp.dma_start(wd2s[:, :], wd2).then_inc(S0["ld"].sem, 16)
            sp.dma_start(wfn[:, :], w_fc).then_inc(S0["ld"].sem, 16)
            sp.dma_start(acol[:, :], w_at[0, D + DE:2 * D + DE].rearrange("(p a) -> p a", a=1)).then_inc(S0["ld"].sem, 16)
            sp.dma_start(asb[:, :], w_at[0:1, 0:D].to_broadcast([P, D])).then_inc(S0["ld"].sem, 16)
            sp.dma_start(be1c[:, :], be1.rearrange("(p a) -> p a", a=1)).then_inc(S0["ld"].sem, 16)
            sp.dma_start(bd1c[:, :], bd1.rearrange("(p a) -> p a", a=1)).then_inc(S0["ld"].sem, 16)
            for row_t, bias in ((b0b, b_l0), (b1b, b_l1), (bd2b, bd2)):
                sp.dma_start(row_t[:, :], bias.rearrange("(a n) -> a n", a=1).to_broadcast([P, D])).then_inc(S0["ld"].sem, 16)
            sp.dma_start(aeb[:, :], w_at[0:1, D:D + DE].to_broadcast([P, DE])).then_inc(S0["ld"].sem, 16)
            sp.wait_ge(S0["pad"].sem, S0["pad"].after(1))
            for h in range(2):
                sp.dma_start(wd1s[h * H2:(h + 1) * H2, h, :], wd1).then_inc(S0["ld"].sem, 16)
            for idx, arr in ((src_i, src), (dst_i, dst), (typ_i, et)):
                sp.dma_start(idx[0:LASTP, 0:T], arr[0:LASTP * T].rearrange("(p t) -> p t", t=T)).then_inc(S0["lde"].sem, 16)
                sp.dma_start(idx[LASTP:P, 0:LASTN], arr[LASTP * T:E].rearrange("(p t) -> p t", p=1)).then_inc(S0["lde"].sem, 16)
            for table in (t_acc, t_x, out):
                sp.dma_start(table[N:NR, :].rearrange("(p c) f -> p (c f)", c=2), zero[:, :]).then_inc(S0["zero"].sem, 16)
            sp.dma_start(t_yacc[N:NR, :].rearrange("(p c) f -> p (c f)", c=2), zero[:, 0:D]).then_inc(S0["zero"].sem, 16)
            sp.wait_ge(S0["zero"].sem, S0["zero"].after(16 * 4))
            sp.wait_ge(S0["ld"].sem, S0["ld"].after(16 * NLD))
            sp.wait_ge(S0["lde"].sem, S0["lde"].after(16 * 6))
            end_phase(sp, SP)
            ln_sync(sp, A0, x)
            end_phase(sp, SP)
            end_phase(sp, SP)

            def conv0_load(r, u, p):
                b = r * SLOTS + u
                if needed(b - SLOTS + 1):
                    sp.wait_ge(L0["xh"].sem, L0["xh"].after(b - SLOTS + 1))
                sp.dma_start(xin[u][0:p], rows_of(x, b, p)).then_inc(L0["ld"][u].sem, 16)
                if needed(b - SLOTS + 1):
                    sp.wait_ge(L0["tr"].sem, L0["tr"].after(b - SLOTS + 1))
                sp.dma_start(ain[u][0:p], rows_of(t_acc, b, p)).then_inc(L0["lda"][u].sem, 16)

            def conv0_store(r, u, p):
                b = r * SLOTS + u
                sp.wait_ge(L0["h1"].sem, L0["h1"].after(b + 1))
                sp.dma_start(rows_of(t_x, b, p), oa[u][0:p]).then_inc(L0["sto"][u].sem, 16)
                sp.dma_start(rows_of(t_h1, b, p), hb[u][0:p]).then_inc(L0["sto"][u].sem, 16)
            node_loop(sp, (conv0_load, 0), (conv0_store, 4))
            stored(sp, L0, 32)
            end_phase(sp, SP)

            def clear(r, u, p):
                b = r * SLOTS + u
                if needed(b):
                    sp.wait_ge(E1["scat"].sem, E1["scat"].after(b * 64))
                sp.dma_start(rows_of(t_acc, b, p), zrow[0:p]).then_inc(E1["zeroed"].sem, 16)
            sp.wait_ge(E1["zrow"].sem, E1["zrow"].after(1))
            node_loop(sp, (clear, 0))
            sp.wait_ge(E1["zeroed"].sem, E1["zeroed"].after(16 * (NB + 1)))
            end_phase(sp, SP)
            end_phase(sp, SP)

            def enc_load(r, u, p):
                b = r * SLOTS + u
                if needed(b - SLOTS + 1):
                    sp.wait_ge(L2["add"].sem, L2["add"].after(b - SLOTS + 1))
                sp.dma_start(xin[u][0:p], rows_of(t_x, b, p)).then_inc(L2["ld"][u].sem, 16)

            def enc_sums(r, u, p):
                b = r * SLOTS + u
                if needed(b - SLOTS + 1):
                    sp.wait_ge(L2["tr"].sem, L2["tr"].after(b - SLOTS + 1))
                sp.dma_start(ain[u][0:p], rows_of(t_acc, b, p)).then_inc(L2["lda"][u].sem, 16)

            def enc_store(r, u, p):
                b = r * SLOTS + u
                sp.wait_ge(L2["y"].sem, L2["y"].after(b + 1))
                sp.dma_start(rows_of(t_y, b, p), yout[u][0:p]).then_inc(L2["sto"][u].sem, 16)
                sp.dma_start(rows_of(t_yacc, b, p), yout[u][0:p]).then_inc(L2["sto"][u].sem, 16)
            node_loop(sp, (enc_load, 0), (enc_sums, 1), (enc_store, 6))
            stored(sp, L2, 32)
            end_phase(sp, SP)
            end_phase(sp, SP)

            def dec_sums(r, u, p):
                b = r * SLOTS + u
                if needed(b - SLOTS + 1):
                    sp.wait_ge(L3["tr"].sem, L3["tr"].after(b - SLOTS + 1))
                sp.dma_start(yin[u][0:p], rows_of(t_yacc, b, p)).then_inc(L3["lda"][u].sem, 16)

            def dec_load(r, u, p):
                b = r * SLOTS + u
                if needed(b - SLOTS + 1):
                    sp.wait_ge(L3["x3"].sem, L3["x3"].after(b - SLOTS + 1))
                sp.dma_start(xin[u][0:p], rows_of(t_x, b, p)).then_inc(L3["ld"][u].sem, 16)

            def dec_store(r, u, p):
                b = r * SLOTS + u
                sp.wait_ge(L3["x3"].sem, L3["x3"].after(b + 1))
                sp.dma_start(rows_of(out, b, p), oa[u][0:p]).then_inc(L3["sto"][u].sem, 16)
            node_loop(sp, (dec_sums, 0), (dec_load, 1), (dec_store, 4))
            stored(sp, L3, 16)
            end_phase(sp, SP)

            def keep_rows(p):
                sp.wait_ge(A3["z"].sem, A3["z"].after(p.q + 1))
                sp.dma_start(t_z[bass.ds(p.q * 2, 2), :, :].rearrange("c p f -> p c f"), tot[:, p.k, :, :]) \
                    .then_inc(A3["sto"][p.k].sem, 16)
            pair_loop(sp, (keep_rows, 0))
            for k in range(RING):
                sp.wait_ge(A3["sto"][k].sem, A3["sto"][k].after(16 * NPAIR // RING))
            end_phase(sp, SP)

            for i in range(4):
                if needed(i - 1):
                    sp.wait_ge(M3["ex"].sem, M3["ex"].after(i - 1))
                sp.dma_start(eas[i % 2][0:LASTP], ea[0:LASTP * T, :].rearrange("(p t) d -> p t d", t=T)
                             [:, i * EH:(i + 1) * EH, :]).then_inc(M3["ld"][i].sem, 16)
                n = min(max(LASTN - i * EH, 0), EH)
                if n:
                    lo = LASTP * T + i * EH
                    sp.dma_start(eas[i % 2][LASTP:P, 0:n, :], ea[lo:lo + n, :].rearrange("(p t) d -> p t d", p=1)) \
                        .then_inc(M3["ld"][i].sem, 16)
                sp.wait_ge(M3["ld"][i].sem, M3["ld"][i].after(32 if n else 16))
            end_phase(sp, SP)

            def load_rows(p):
                if needed(p.q - RING + 1):
                    sp.wait_ge(B3["scat"].sem, B3["scat"].after((p.q - RING + 1) * 32))
                sp.dma_start(g[:, p.k, :, :], t_z[bass.ds(p.q * 2, 2), :, :].rearrange("c p f -> p c f")) \
                    .then_inc(B3["load"][p.k].sem, 16)
            pair_loop(sp, (load_rows, 0))
            end_phase(sp, SP)

        @block.gpsimd
        def _(gp):
            gp.memset(ident[:, :], 0.0).then_inc(S0["made"].sem, 1)
            gp.memset(ones[:, :], 1.0).then_inc(S0["made"].sem, 1)
            gp.memset(earlier[:, :, :], 1.0).then_inc(S0["made"].sem, 1)
            gp.memset(zero[:, :], 0.0)
            gp.memset(zero16[:, :], 0.0)
            gp.memset(wd1s[:, :, :], 0.0)
            gp.memset(src_i[:, :], 0)
            gp.memset(dst_i[:, :], 0)
            gp.memset(typ_i[:, :], 0).then_inc(S0["pad"].sem, 1)
            gp.iota(ioc[:, :], [[1, NC]], base=0, channel_multiplier=0, allow_small_or_imprecise_dtypes=True)
            gp.iota(iop[:, :], [[1, P]], base=0, channel_multiplier=0, allow_small_or_imprecise_dtypes=True)
            gp.iota(spare[:, :], [[P, 2]], base=N, channel_multiplier=1, allow_small_or_imprecise_dtypes=True)
            gp.wait_ge(S0["made"].sem, S0["made"].after(3))
            gp.affine_select(out=ident[:, :], in_=ident[:, :], compare_op=ALU.not_equal, fill=1.0, base=0,
                             pattern=[[-1, P]], channel_multiplier=1)
            i = gp.affine_select(out=earlier[:, :, :], in_=earlier[:, :, :], compare_op=ALU.is_gt, fill=0.0, base=0,
                                 pattern=[[P, 2], [-1, 2 * P]], channel_multiplier=1)
            i.then_inc(S0["made"].sem, 1)
            gp.wait_ge(S0["calc"].sem, S0["calc"].after(1))
            for f in (src_f, dst_f):
                i = gp.affine_select(out=f[:, 0:T], in_=f[:, 0:T], compare_op=ALU.is_ge, fill=float(N + LASTP), base=E - 1,
                                     pattern=[[-1, T]], channel_multiplier=-T)
            i.then_inc(S0["made"].sem, 1)
            end_phase(gp, PO)
            end_phase(gp, PO)
            edge_pool(gp, E0, t_src, t_acc, tot, g)
            end_phase(gp, PO)

            def conv0_xh(r, u, p):
                b = r * SLOTS + u
                gp.wait_ge(L0["h"].sem, L0["h"].after(b + 1))
                gp.tensor_tensor(ob_h[u][0:p], xin[u][0:p], ob_h[u][0:p], ALU.add).then_inc(L0["xh"].sem, 1)
            node_loop(gp, (conv0_xh, 0))
            end_phase(gp, PO)
            edge_pool(gp, E1, t_h1, t_x, tot, gn)
            end_phase(gp, PO)
            edge_pool(gp, E2, t_x, t_acc, tot, g)
            end_phase(gp, PO)

            def enc_add(r, u, p):
                b = r * SLOTS + u
                gp.wait_ge(L2["h"].sem, L2["h"].after(b + 1))
                gp.wait_ge(L2["lda"][u].sem, L2["lda"][u].after(r * 16 + 16))
                gp.tensor_tensor(ain[u][0:p], ain[u][0:p], xin[u][0:p], ALU.add).then_inc(L2["add"].sem, 1)
            node_loop(gp, (enc_add, 0))
            end_phase(gp, PO)
            edge_pool(gp, E3, t_y, t_yacc, toty, gy)
            end_phase(gp, PO)

            def dec_xb(r, u, p):
                b = r * SLOTS + u
                gp.wait_ge(L3["ld"][u].sem, L3["ld"][u].after(r * 16 + 16))
                gp.tensor_tensor(xin[u][0:p], xin[u][0:p], bd2b[0:p, :].rearrange("p (a f) -> p a f", a=1)
                                 .to_broadcast([p, K, D]), ALU.add).then_inc(L3["xb"].sem, 1)
            node_loop(gp, (dec_xb, 0))
            end_phase(gp, PO)

            def edge_rows(p):
                gp.wait_ge(A3["ring"].sem, A3["ring"].after(p.q + 1))
                gp.sem_inc(tick, 1)
                for c in range(2):
                    gp.indirect_dma_start(g[:, p.k, c, :], None, out,
                                          bass.IndirectOffsetOnAxis(ap=gidx[:, p.k, c:c + 1], axis=0)) \
                        .then_inc(A3["gath"][p.k].sem, 16)
                    gp.indirect_dma_start(gd[:, p.k, c, :], None, out,
                                          bass.IndirectOffsetOnAxis(ap=didx[:, p.k, c:c + 1], axis=0)) \
                        .then_inc(A3["gath"][p.k].sem, 16)
            pair_loop(gp, (edge_rows, 0))
            end_phase(gp, PO)
            end_phase(gp, PO)
            edge_pool(gp, B3, None, out, tot)
            end_phase(gp, PO)

        def softmax(v):
            n_v, turn = [0], [0]

            def link(i):
                n_v[0] += 1
                i.then_inc(M3["v"].sem, 1)
                v.wait_ge(M3["v"].sem, M3["v"].after(n_v[0]))
            vec = nc.vector
            link(vec.memset(alpha[:, :], 0.0))
            link(vec.memset(se[:, :], 0.0))
            for i in range(4):
                n = min(max(LASTN - i * EH, 0), EH)
                v.wait_ge(M3["ld"][i].sem, M3["ld"][i].after(32 if n else 16))
                link(vec.tensor_tensor(prod[0:LASTP], eas[i % 2][0:LASTP], aeb[0:LASTP, :].rearrange("p (a d) -> p a d", a=1)
                                       .to_broadcast([LASTP, EH, DE]), ALU.mult))
                link(vec.tensor_reduce(se[0:LASTP, i * EH:(i + 1) * EH], prod[0:LASTP], AX.X, ALU.add))
                if n:
                    link(vec.tensor_tensor(prod[96:P, 0:n], eas[i % 2][96:P, 0:n], aeb[96:P, :]
                                           .rearrange("p (a d) -> p a d", a=1).to_broadcast([P - 96, n, DE]), ALU.mult))
                    link(vec.tensor_reduce(se[96:P, i * EH:i * EH + n], prod[96:P, 0:n], AX.X, ALU.add))
                v.sem_inc(M3["ex"].sem, 1)
            link(vec.tensor_tensor(se[:, :], se[:, :], e_[:, 0:T], ALU.add))
            link(vec.scalar_tensor_tensor(out=e_[:, 0:T], in0=se[:, :], scalar=0.01, in1=se[:, :], op0=ALU.mult, op1=ALU.max))
            link(vec.memset(same[:, :], 1.0))
            link(vec.memset(gsame[:, :], 1.0))
            link(vec.tensor_tensor(same[:, 1:T], dst_f[:, 1:T], dst_f[:, 0:T - 1], ALU.is_equal))
            link(vec.tensor_scalar(gsame[:, 0:T - 1], same[:, 1:T], 1.0, None, ALU.mult))
            link(vec.tensor_scalar(nsame[:, :], same[:, :], -1.0, BIG, ALU.add, ALU.mult))
            link(vec.tensor_scalar(gnot[:, :], gsame[:, :], -1.0, 1.0, ALU.mult, ALU.add))
            def row_step(name, column):
                n = turn[0]
                assert TURNS[n] == "row"
                turn[0] += 1
                vec.tensor_copy(col[:, n:n + 1], column).then_inc(M3["ready"].sem, 1)
                v.wait_ge(M3["pe"].sem, M3["pe"].after(n + 1))
                link(vec.tensor_copy(names[name], ps[0:1, 0:P]))

            def col_step(column):
                n = turn[0]
                assert TURNS[n] == "col"
                turn[0] += 1
                vec.tensor_copy(names["turned"], names["turn"]).then_inc(M3["ready"].sem, 1)
                v.wait_ge(M3["pe"].sem, M3["pe"].after(n + 1))
                link(vec.tensor_copy(column, ps[:, 0:1]))
            row_step("first", dst_f[:, 0:1])
            row_step("last", dst_f[:, T - 1:T])
            R_ = names
            link(vec.memset(R_["contp"], 0.0))
            link(vec.memset(R_["contn"], 0.0))
            link(vec.tensor_tensor(R_["contp"][:, 1:P], R_["first"][:, 1:P], R_["last"][:, 0:P - 1], ALU.is_equal))
            link(vec.tensor_tensor(R_["contn"][:, 0:P - 1], R_["first"][:, 1:P], R_["last"][:, 0:P - 1], ALU.is_equal))
            link(vec.tensor_tensor(R_["single"], R_["first"], R_["last"], ALU.is_equal))
            link(vec.tensor_scalar(R_["cinn"], R_["contp"], -1.0, BIG, ALU.add, ALU.mult))

            def back_fill(values, out_t):
                link(vec.tensor_tensor(tcv[:, :], gnot[:, :], values, ALU.mult))
                link(vec.tensor_scalar(ta[:, :], gsame[:, :], 1.0, None, ALU.mult))
                link(vec.memset(ta[:, T - 1:T], 0.0))
                link(vec.tensor_scalar(tcv[:, T - 1:T], values[:, T - 1:T], 1.0, None, ALU.mult))
                link(vec.tensor_tensor_scan(out_t[:, ::-1], ta[:, ::-1], tcv[:, ::-1], 0.0, ALU.mult, ALU.add))
                row_step("t", out_t[:, 0:1])
                row_step("base", values[:, T - 1:T])
                link(vec.tensor_tensor(R_["dn"], R_["single"], R_["contn"], ALU.mult))
                link(vec.tensor_scalar(R_["turn"], R_["dn"], -1.0, 1.0, ALU.mult, ALU.add))
                link(vec.tensor_tensor(R_["turn"], R_["turn"], R_["t"], ALU.mult))
                link(vec.tensor_tensor_scan(R_["scan"][:, ::-1], R_["dn"][:, ::-1], R_["turn"][:, ::-1], 0.0, ALU.mult, ALU.add))
                link(vec.tensor_scalar(R_["turn"], R_["contn"], -1.0, 1.0, ALU.mult, ALU.add))
                link(vec.tensor_tensor(R_["turn"], R_["turn"], R_["base"], ALU.mult))
                link(vec.tensor_tensor(R_["neg"][:, 0:P - 1], R_["contn"][:, 0:P - 1], R_["scan"][:, 1:P], ALU.mult))
                link(vec.tensor_tensor(R_["turn"][:, 0:P - 1], R_["turn"][:, 0:P - 1], R_["neg"][:, 0:P - 1], ALU.add))
                col_step(col2[:, 0:1])
                link(vec.tensor_tensor(tcv[:, :], gnot[:, :], values, ALU.mult))
                link(vec.tensor_tensor_scan(out_t[:, ::-1], gsame[:, ::-1], tcv[:, ::-1], col2[:, 0:1], ALU.mult, ALU.add))

            link(vec.tensor_scalar(tb[:, :], nsame[:, :], 1.0, None, ALU.mult))
            link(vec.memset(tb[:, 0:1], 0.0))
            link(vec.tensor_tensor_scan(fwd[:, :], tb[:, :], e_[:, 0:T], -BIG, ALU.add, ALU.max))
            row_step("t", fwd[:, T - 1:T])
            link(vec.tensor_tensor(R_["dn"], R_["single"], R_["contp"], ALU.mult))
            link(vec.tensor_scalar(R_["dn"], R_["dn"], -1.0, BIG, ALU.add, ALU.mult))
            link(vec.tensor_tensor_scan(R_["scan"], R_["dn"], R_["t"], -BIG, ALU.add, ALU.max))
            link(vec.memset(R_["turn"], -BIG))
            link(vec.tensor_tensor(R_["turn"][:, 1:P], R_["scan"][:, 0:P - 1], R_["cinn"][:, 1:P], ALU.add))
            col_step(col2[:, 1:2])
            link(vec.tensor_tensor_scan(fwd[:, :], tb[:, :], e_[:, 0:T], col2[:, 1:2], ALU.add, ALU.max))
            back_fill(fwd[:, :], bwd)
            vec.tensor_tensor(wgt[:, :], e_[:, 0:T], bwd[:, :], ALU.subtract).then_inc(M3["diff"].sem, 1)
            v.wait_ge(M3["exp"].sem, M3["exp"].after(1))
            link(vec.tensor_scalar(tb[:, :], same[:, :], 1.0, None, ALU.mult))
            link(vec.tensor_tensor_scan(fwd[:, :], tb[:, :], wgt[:, :], 0.0, ALU.mult, ALU.add))
            row_step("t", fwd[:, T - 1:T])
            link(vec.tensor_tensor(R_["dn"], R_["single"], R_["contp"], ALU.mult))
            link(vec.tensor_tensor_scan(R_["scan"], R_["dn"], R_["t"], 0.0, ALU.mult, ALU.add))
            link(vec.memset(R_["turn"], 0.0))
            link(vec.tensor_tensor(R_["turn"][:, 1:P], R_["scan"][:, 0:P - 1], R_["contp"][:, 1:P], ALU.mult))
            col_step(col2[:, 2:3])
            link(vec.tensor_tensor_scan(fwd[:, :], tb[:, :], wgt[:, :], col2[:, 2:3], ALU.mult, ALU.add))
            back_fill(fwd[:, :], bwd)
            link(vec.tensor_scalar(ta[:, :], bwd[:, :], 0.0, None, ALU.is_le))
            link(vec.tensor_tensor(bwd[:, :], bwd[:, :], ta[:, :], ALU.add))
            link(vec.reciprocal(bwd[:, :], bwd[:, :]))
            link(vec.tensor_tensor(alpha[:, 0:T], wgt[:, :], bwd[:, :], ALU.mult))

        @block.vector
        def _(v):
            done = [0]

            def link(i, sem=S0["deg"]):
                done[0] += 1
                i.then_inc(sem.sem, 1)
                v.wait_ge(sem.sem, sem.after(done[0]))

            v.wait_ge(S0["lde"].sem, S0["lde"].after(16 * 6))
            for f, i32 in ((src_f, src_i), (dst_f, dst_i), (typ_f, typ_i)):
                i = nc.vector.tensor_copy(f[:, :], i32[:, :])
            i.then_inc(S0["calc"].sem, 1)
            v.wait_ge(S0["made"].sem, S0["made"].after(5))
            for f, hp, hc in ((src_f, hpar[0], hcol[0]), (dst_f, hpar[1], hcol[1])):
                def floor_div(out_t, in_t, n):
                    link(nc.vector.tensor_scalar(out_t, in_t, 1.0 / n, 0.5 / n - 0.5, ALU.mult, ALU.add))
                    link(nc.vector.tensor_scalar(out_t, out_t, ROUND, None, ALU.add))
                    link(nc.vector.tensor_scalar(out_t, out_t, -ROUND, None, ALU.add))
                floor_div(ta[:, :], f[:, 0:T], BR)
                link(nc.vector.scalar_tensor_tensor(out=tb[:, :], in0=ta[:, :], scalar=-float(BR), in1=f[:, 0:T],
                                                    op0=ALU.mult, op1=ALU.add))
                floor_div(hp[:, :], tb[:, :], K)
                link(nc.vector.scalar_tensor_tensor(out=tb[:, :], in0=hp[:, :], scalar=-float(K), in1=tb[:, :],
                                                    op0=ALU.mult, op1=ALU.add))
                link(nc.vector.scalar_tensor_tensor(out=hc[:, :], in0=ta[:, :], scalar=float(K), in1=tb[:, :],
                                                    op0=ALU.mult, op1=ALU.add))
            def hot(pair):
                for c in range(2):
                    t = pair.q * 2 + c
                    slot = pair.w * 2 + c
                    if needed(t - 3):
                        v.wait_ge(S0["mm"].sem, S0["mm"].after(t - 3))
                    nc.vector.tensor_scalar(oneh_p[:, slot, :], iop[:, :], hpar[0][:, bass.ds(t, 1)], None, ALU.is_equal)
                    nc.vector.tensor_scalar(oneh_c[:, slot, :], ioc[:, :], hcol[0][:, bass.ds(t, 1)], None, ALU.is_equal) \
                        .then_inc(S0["hot"].sem, 1)
            pair_loop(v, (hot, 0))
            v.wait_ge(S0["mm"].sem, S0["mm"].after(T + 1))
            for j in range(2):
                lo = j * NC // 2
                link(nc.vector.tensor_scalar(dis[0][:, lo:lo + NC // 2], ps[:, j * 512:j * 512 + NC // 2],
                                             1.0, None, ALU.add))
            nc.vector.tensor_copy(w0t[:, :], ps[:, 2048:2048 + D])
            nc.vector.tensor_copy(wft[:, :], ps[:, 2048 + D:2048 + 2 * D])
            nc.vector.tensor_copy(vdb[:, :], ps[:, 2048 + 2 * D:2048 + 3 * D])
            v.wait_ge(S0["root"].sem, S0["root"].after(1))
            link(nc.vector.reciprocal(dis[0][:, :], dis[0][:, :]))
            end_phase(v, VE)
            ln_vector(v, A0, dis[0])
            end_phase(v, VE)

            def target_hot(pair):
                if needed(pair.q - 1):
                    v.wait_ge(E0["count"].sem, E0["count"].after(pair.q - 1))
                for c in range(2):
                    t, slot = pair.q * 2 + c, pair.w * 2 + c
                    nc.vector.tensor_scalar(oneh_p[:, slot, :], iop[:, :], hpar[1][:, bass.ds(t, 1)], None, ALU.is_equal)
                    i = nc.vector.tensor_scalar(oneh_c[:, slot, :], ioc[:, :], hcol[1][:, bass.ds(t, 1)], None, ALU.is_equal)
                i.then_inc(E0["hot"].sem, 1)
            edge_vector(v, E0, dst_i, src_f, between=target_hot)
            v.wait_ge(C0["close"].sem, C0["close"].after(1))
            for j in range(2):
                lo = j * NC // 2
                i = nc.vector.tensor_scalar(dis[1][:, lo:lo + NC // 2], ps[:, CNT + j * 512:CNT + j * 512 + NC // 2],
                                            1.0, None, ALU.add)
            i.then_inc(C0["v"].sem, 1)
            v.wait_ge(C0["root"].sem, C0["root"].after(1))
            nc.vector.reciprocal(dis[1][:, :], dis[1][:, :])
            end_phase(v, VE)

            def conv0_slot(r, u, p):
                b = r * SLOTS + u
                if needed(b - SLOTS + 1):
                    v.wait_ge(L0["h"].sem, L0["h"].after(b - SLOTS + 1))
                for slot, kept in ((sc, rstd_r), (nbi, mean_r)):
                    i = nc.vector.tensor_scalar(slot[0:p, u, :], kept[0:p, bass.ds(b * K, K)], 1.0, None, ALU.mult)
                i.then_inc(L0["sc"].sem, 1)

            def conv0_rest(r, u, p):
                b = r * SLOTS + u
                if needed(r * 32):
                    v.wait_ge(L0["sto"][u].sem, L0["sto"][u].after(r * 32))
                nc.vector.tensor_scalar(dz[0:p, u, :], dis[0][0:p, bass.ds(b * K, K)], 1.0, None, ALU.mult) \
                    .then_inc(L0["dz"].sem, 1)
                nc.vector.tensor_scalar(hb[u][0:p, :, D], dis[1][0:p, bass.ds(b * K, K)], 1.0, None, ALU.mult)
                v.wait_ge(L0["dz"].sem, L0["dz"].after(b + 1))
                v.wait_ge(L0["mm"].sem, L0["mm"].after(b + 1))
                for k in range(K):
                    i = nc.vector.scalar_tensor_tensor(out=oa[u][0:p, k, :], in0=ps[0:p, ZC + k * P:ZC + (k + 1) * P],
                                                       scalar=dz[0:p, u, k:k + 1], in1=b0b[0:p, :], op0=ALU.mult,
                                                       op1=ALU.add)
                i.then_inc(L0["z"].sem, 1)
                v.wait_ge(L0["z"].sem, L0["z"].after(b + 1))
                v.wait_ge(L0["xh"].sem, L0["xh"].after(b + 1))
                nc.vector.scalar_tensor_tensor(out=oa[u][0:p], in0=oa[u][0:p], scalar=0.0, in1=ob_h[u][0:p],
                                               op0=ALU.max, op1=ALU.add).then_inc(L0["res"].sem, 1)
                v.wait_ge(L0["res"].sem, L0["res"].after(b + 1))
                stats(v, L0, b, u, p, oa[u], dis[0])
            node_loop(v, (conv0_slot, 0), (row_scales(v, L0), 2), (conv0_rest, 1))
            end_phase(v, VE)

            def type_ring(p):
                nc.vector.tensor_scalar(typr[:, p.k, :], typ_f[:, bass.ds(p.q * 2, 2)], 1.0, None, ALU.mult)

            def mask(p):
                if needed(p.q - 1):
                    v.wait_ge(E1["xw"].sem, E1["xw"].after(p.q - 1))
                v.wait_ge(E1["txc"].sem, E1["txc"].after(p.q + 1))
                nc.vector.tensor_scalar(nsrc[:, bass.ds(p.q * 2, 2)], gn[:, p.k, :, D], 1.0, None, ALU.mult)
                for k in range(R):
                    i = nc.vector.scalar_tensor_tensor(out=xm[:, p.w, k, :], in0=xT[:, p.w, 2 * P:4 * P], scalar=float(k),
                                                       in1=xT[:, p.w, 0:2 * P], op0=ALU.is_equal, op1=ALU.mult)
                i.then_inc(E1["masked"].sem, 1)

            nc.vector.memset(zrow, 0.0).then_inc(E1["zrow"].sem, 1)
            edge_vector(v, E1, src_i, dst_f, type_ring, mask)
            end_phase(v, VE)

            def e2_stats(p):
                v.wait_ge(E2["gath"][p.k].sem, E2["gath"][p.k].after(p.n * 32 + 32))
                edge_stats(v, E2, p, [g[:, p.k, c, :] for c in range(2)], e2_norms)

            def e2_norms(p):
                nc.vector.tensor_scalar(enorm[:, p.w, :], nsrc[:, bass.ds(p.q * 2, 2)], 1.0, None, ALU.mult)

            def e2_scales(p):
                edge_scales(v, E2, p, 2)
                nc.vector.tensor_tensor(esc[:, p.w, 0:2], ers[:, p.w, 0:2], enorm[:, p.w, :], ALU.mult) \
                    .then_inc(E2["sc"].sem, 1)
                v.wait_ge(E2["sc"].sem, E2["sc"].after(p.q + 1))
                edge_bias(E2, p, 2, esc)
            edge_vector(v, E2, src_i, dst_f, None, e2_stats, e2_scales)
            end_phase(v, VE)

            def enc_stats(r, u, p):
                b = r * SLOTS + u
                if needed(b - SLOTS + 1):
                    v.wait_ge(L2["scal"].sem, L2["scal"].after(b - SLOTS + 1))
                v.wait_ge(L2["ld"][u].sem, L2["ld"][u].after(r * 16 + 16))
                stats(v, L2, b, u, p, xin[u], dis[1])

            def enc_h_scales(r, u, p):
                b = r * SLOTS + u
                rstd(v, L2, b, p)
                if needed(b - SLOTS + 1):
                    v.wait_ge(L2["h"].sem, L2["h"].after(b - SLOTS + 1))
                nc.vector.tensor_tensor(sc[0:p, u, :], rs[0:p, :], dsl[0:p, u, :], ALU.mult).then_inc(L2["sc"].sem, 1)
                v.wait_ge(L2["sc"].sem, L2["sc"].after(b + 1))
                nc.vector.scalar_tensor_tensor(out=nbi[0:p, u, :], in0=mv[0:p, :, 0], scalar=-1.0, in1=sc[0:p, u, :],
                                               op0=ALU.mult, op1=ALU.mult).then_inc(L2["nb"].sem, 1)

            def enc_scale(r, u, p):
                b = r * SLOTS + u
                v.wait_ge(L2["add"].sem, L2["add"].after(b + 1))
                nc.vector.tensor_tensor(ain[u][0:p], ain[u][0:p], norm_of(u, p, D), ALU.mult).then_inc(L2["scal"].sem, 1)

            def norm_of(u, p, width, slot=dsl):
                return slot[0:p, u, :].rearrange("p (k a) -> p k a", a=1).to_broadcast([p, K, width])

            def enc_y(r, u, p):
                b = r * SLOTS + u
                if needed(r * 32):
                    v.wait_ge(L2["sto"][u].sem, L2["sto"][u].after(r * 32))
                nc.vector.tensor_scalar(dz[0:p, u, :], dis[1][0:p, bass.ds(b * K, K)], 1.0, None, ALU.mult) \
                    .then_inc(L2["dz"].sem, 1)
                v.wait_ge(L2["dz"].sem, L2["dz"].after(b + 1))
                v.wait_ge(L2["mm2"].sem, L2["mm2"].after(b + 1))
                nc.vector.tensor_tensor(yout[u][0:p], ps[0:p, 3072:3072 + K * H2].rearrange("p (k f) -> p k f", k=K),
                                        norm_of(u, p, H2, dz), ALU.mult).then_inc(L2["y"].sem, 1)
            node_loop(v, (enc_stats, 0), (enc_scale, 2), (enc_h_scales, 0), (enc_y, 5))
            end_phase(v, VE)
            edge_vector(v, E3, src_i, dst_f)
            end_phase(v, VE)

            def dec_scale(r, u, p):
                b = r * SLOTS + u
                nc.vector.tensor_scalar(dz[0:p, u, :], dis[1][0:p, bass.ds(b * K, K)], 1.0, None, ALU.mult) \
                    .then_inc(L3["sc"].sem, 1)
                v.wait_ge(L3["sc"].sem, L3["sc"].after(b + 1))
                v.wait_ge(L3["lda"][u].sem, L3["lda"][u].after(r * 16 + 16))
                nc.vector.tensor_tensor(yin[u][0:p], yin[u][0:p], dz[0:p, u, :].rearrange("p (k a) -> p k a", a=1)
                                        .to_broadcast([p, K, H2]), ALU.mult).then_inc(L3["scal"].sem, 1)
            def dec_x3(r, u, p):
                b = r * SLOTS + u
                if needed(r * 16):
                    v.wait_ge(L3["sto"][u].sem, L3["sto"][u].after(r * 16))
                v.wait_ge(L3["d2"].sem, L3["d2"].after(b + 1))
                v.wait_ge(L3["xb"].sem, L3["xb"].after(b + 1))
                for h in range(2):
                    nc.vector.tensor_tensor(oa[u][0:p, h:8:2, :], dec_view[0:p, 4 * h:4 * h + 4, :],
                                            xin[u][0:p, h:8:2, :], ALU.add)
                nc.vector.tensor_tensor(oa[u][0:p, 8:K, :], dec_view[0:p, 8:K, :], xin[u][0:p, 8:K, :], ALU.add) \
                    .then_inc(L3["x3"].sem, 1)
            node_loop(v, (dec_scale, 0), (dec_x3, 3))
            end_phase(v, VE)

            def score_ring(p):
                if needed(p.n):
                    v.wait_ge(A3["sto"][p.k].sem, A3["sto"][p.k].after(p.n * 16))
                nc.vector.tensor_scalar(gidx[:, p.k, :], src_i[:, bass.ds(p.q * 2, 2)], 1.0, None, ALU.mult)
                nc.vector.tensor_scalar(didx[:, p.k, :], dst_i[:, bass.ds(p.q * 2, 2)], 1.0, None, ALU.mult) \
                    .then_inc(A3["ring"].sem, 1)
            for q in range(SCORE_AHEAD):
                score_ring(Pair(0, q))

            def scores(p):
                v.wait_ge(A3["z"].sem, A3["z"].after(p.q + 1))
                if needed(p.q - 1):
                    v.wait_ge(A3["e"].sem, A3["e"].after(p.q - 1))
                for c in range(2):
                    for n, (rows, other) in enumerate(((tot, asb), (gd, vdb))):
                        i = nc.vector.tensor_tensor_reduce(out=junk[:, n, c * P:(c + 1) * P], in0=rows[:, p.k, c, :],
                                                           in1=other[:, :], scale=1.0, scalar=0.0, op0=ALU.mult,
                                                           op1=ALU.add, accum_out=sco[:, p.w, n, c:c + 1])
                i.then_inc(A3["dot"].sem, 1)
                v.wait_ge(A3["dot"].sem, A3["dot"].after(p.q + 1))
                nc.vector.tensor_tensor(e_[:, bass.ds(p.q * 2, 2)], sco[:, p.w, 0, :], sco[:, p.w, 1, :], ALU.add) \
                    .then_inc(A3["e"].sem, 1)

            def score_stats(p):
                v.wait_ge(A3["gath"][p.k].sem, A3["gath"][p.k].after(p.n * 64 + 64))
                edge_stats(v, A3, p, [t[:, p.k, c, :] for t in (g, gd) for c in range(2)],
                           lambda p: score_ring(p.plus(SCORE_AHEAD)))

            def score_scales(p):
                edge_scales(v, A3, p, 4)
                edge_bias(A3, p, 4, ers)
            pair_loop(v, (scores, 4), (score_stats, 0), (score_scales, 1))
            end_phase(v, VE)
            softmax(v)
            end_phase(v, VE)

            def alpha_ring(p):
                nc.vector.tensor_scalar(alr[:, p.k, :], alpha[:, bass.ds(p.q * 2, 2)], 1.0, None, ALU.mult)
            edge_vector(v, B3, src_i, dst_f, alpha_ring)
            end_phase(v, VE)

        @block.tensor
        def _(pe):
            pe.wait_ge(S0["made"].sem, S0["made"].after(5))
            pe.wait_ge(S0["ld"].sem, S0["ld"].after(16 * NLD))
            nc.tensor.transpose(ps[:, 2048:2048 + D], wn[:, :], ident[:, :])
            nc.tensor.transpose(ps[:, 2048 + D:2048 + 2 * D], wfn[:, :], ident[:, :])
            nc.tensor.matmul(ps[:, 2048 + 2 * D:2048 + 3 * D], acol[:, :].to_broadcast([D, P]), wfn[:, :],
                             start=True, stop=True)

            def counts(slot, o, first):
                for j in range(2):
                    i = nc.tensor.matmul(ps[:, o + j * 512:o + j * 512 + NC // 2], oneh_p[:, slot, :],
                                         oneh_c[:, slot, j * NC // 2:(j + 1) * NC // 2], start=first, stop=False)
                return i

            def close_counts(o):
                for j in range(2):
                    i = nc.tensor.matmul(ps[:, o + j * 512:o + j * 512 + NC // 2], zero16[:, :],
                                         oneh_c[:, 0, j * NC // 2:(j + 1) * NC // 2], start=False, stop=True)
                return i

            def count(p):
                for c in range(2):
                    t = p.q * 2 + c
                    pe.wait_ge(S0["hot"].sem, S0["hot"].after(t + 1))
                    counts(p.w * 2 + c, 0, isinstance(t, int) and t == 0).then_inc(S0["mm"].sem, 1)
            pair_loop(pe, (count, 0))
            close_counts(0).then_inc(S0["mm"].sem, 1)
            end_phase(pe, PE)
            end_phase(pe, PE)

            def target_count(p):
                pe.wait_ge(E0["hot"].sem, E0["hot"].after(p.q + 1))
                for c in range(2):
                    i = counts(p.w * 2 + c, CNT, isinstance(p.q, int) and p.q == 0 and c == 0)
                i.then_inc(E0["count"].sem, 1)

            edge_tensor(pe, E0, D, gathered(pe, E0), g, RING, after=target_count)
            close_counts(CNT).then_inc(C0["close"].sem, 1)
            end_phase(pe, PE)

            def conv0_turn(r, u, p):
                b = r * SLOTS + u
                pe.wait_ge(L0["lda"][u].sem, L0["lda"][u].after(r * 16 + 16))
                if needed(b):
                    pe.wait_ge(L0["trc"].sem, L0["trc"].after(b))
                for k in range(K):
                    i = nc.tensor.transpose(ps[:, k * P:k * P + p], ain[u][0:p, k, :], ident[0:p, 0:p])
                i.then_inc(L0["tr"].sem, 1)

            def conv0_mm(r, u, p):
                b = r * SLOTS + u
                pe.wait_ge(L0["trc"].sem, L0["trc"].after(b + 1))
                if needed(b):
                    pe.wait_ge(L0["z"].sem, L0["z"].after(b))
                for k in range(K):
                    i = nc.tensor.matmul(ps[0:p, ZC + k * P:ZC + (k + 1) * P], fT[u][:, k, 0:p], w0t[:, :],
                                         start=True, stop=True)
                i.then_inc(L0["mm"].sem, 1)
            node_loop(pe, (conv0_turn, 0), (conv0_mm, 1))
            end_phase(pe, PE)

            def turn(p):
                pe.wait_ge(E1["gath"][p.k].sem, E1["gath"][p.k].after(p.n * 32 + 32))
                if needed(p.q - 1):
                    pe.wait_ge(E1["txc"].sem, E1["txc"].after(p.q - 1))
                for c in range(2):
                    o = TURN[p.w] + c * P
                    nc.tensor.transpose(ps[:, o:o + P], gn[:, p.k, c, 0:D], ident[:, :])
                for c in range(2):
                    o = TURN[p.w] + (2 + c) * P
                    i = nc.tensor.transpose(ps[:, o:o + P], typr[:, p.k, c:c + 1].to_broadcast([P, P]), ident[:, :])
                i.then_inc(E1["tx"].sem, 1)

            def products(p):
                pe.wait_ge(E1["masked"].sem, E1["masked"].after(p.q + 1))
                if needed(p.q - 1):
                    pe.wait_ge(E1["relu"].sem, E1["relu"].after(p.q - 1))
                for c in range(2):
                    o = XW + p.w * 512 + c * P
                    nc.tensor.matmul(ps[:, o:o + P], ones[0:1, :], b1b[0:1, :], start=True, stop=False)
                    for k in range(R):
                        i = nc.tensor.matmul(ps[:, o:o + P], xm[:, p.w, k, c * P:(c + 1) * P], w1[:, k, :],
                                             start=False, stop=(k == R - 1))
                i.then_inc(E1["xw"].sem, 1)

            def e1_start():
                turn(Pair(0, 0))
                turn(Pair(0, 1))
                products(Pair(0, 0))

            def turn_ahead(p):
                turn(p.plus(2))

            def products_ahead(p):
                products(p.plus(1))

            def relu_ready(p):
                pe.wait_ge(E1["relu"].sem, E1["relu"].after(p.q + 1))
            edge_tensor(pe, E1, D, relu_ready, msg, 2, e1_start, turn_ahead, products_ahead)
            end_phase(pe, PE)

            def h_ready(p):
                pe.wait_ge(E2["h"].sem, E2["h"].after(p.q + 1))
            edge_tensor(pe, E2, D, h_ready, msg, 2)
            end_phase(pe, PE)

            def groups(p):
                return [(0, 4), (4, 8), (8, K)]

            def enc_turn(r, u, p):
                b = r * SLOTS + u
                pe.wait_ge(L2["scal"].sem, L2["scal"].after(b + 1))
                if needed(b):
                    pe.wait_ge(L2["trc"].sem, L2["trc"].after(b))
                for k in range(K):
                    i = nc.tensor.transpose(ps[:, k * P:k * P + p], ain[u][0:p, k, :], ident[0:p, 0:p])
                i.then_inc(L2["tr"].sem, 1)

            def enc_mm(r, u, p):
                b = r * SLOTS + u
                pe.wait_ge(L2["trc"].sem, L2["trc"].after(b + 1))
                if needed(b):
                    pe.wait_ge(L2["relu"].sem, L2["relu"].after(b))
                for lo, hi in groups(p):
                    i = nc.tensor.matmul(zc_view[:, lo:hi, 0:p], we1s[:, :], fT[u][:, lo:hi, 0:p], start=True, stop=True)
                i.then_inc(L2["mm"].sem, 1)

            def enc_mm2(r, u, p):
                b = r * SLOTS + u
                pe.wait_ge(L2["relu"].sem, L2["relu"].after(b + 1))
                if needed(b):
                    pe.wait_ge(L2["y"].sem, L2["y"].after(b))
                for k in range(K):
                    i = nc.tensor.matmul(ps[0:p, 3072 + k * H2:3072 + (k + 1) * H2], tT[u][:, k, 0:p], we2s[:, :],
                                         start=True, stop=True)
                i.then_inc(L2["mm2"].sem, 1)
            node_loop(pe, (enc_turn, 0), (enc_mm, 1), (enc_mm2, 2))
            end_phase(pe, PE)
            edge_tensor(pe, E3, H2, gathered(pe, E3), gy, RING)
            end_phase(pe, PE)

            def dec_turn(r, u, p):
                b = r * SLOTS + u
                pe.wait_ge(L3["scal"].sem, L3["scal"].after(b + 1))
                if needed(b):
                    pe.wait_ge(L3["trc"].sem, L3["trc"].after(b))
                for j in range(K // 2):
                    i = nc.tensor.transpose(ps[:, j * P:j * P + p], yin[u][0:p, 2 * j:2 * j + 2, :]
                                            .rearrange("p k f -> p (k f)"), ident[0:p, 0:p])
                i.then_inc(L3["tr"].sem, 1)

            def dec_hidden(r, u, p):
                b = r * SLOTS + u
                pe.wait_ge(L3["trc"].sem, L3["trc"].after(b + 1))
                if needed(b):
                    pe.wait_ge(L3["d1c"].sem, L3["d1c"].after(b))
                for h in range(2):
                    for lo, hi in ((0, 4), (4, K // 2)):
                        o = 4 * h if lo == 0 else 8 + h
                        i = nc.tensor.matmul(hid_view[:, o:o + hi - lo, 0:p], wd1s[:, h, :], tT[u][:, lo:hi, 0:p],
                                             start=True, stop=True)
                i.then_inc(L3["d1"].sem, 1)

            def dec_out(r, u, p):
                b = r * SLOTS + u
                pe.wait_ge(L3["d1c"].sem, L3["d1c"].after(b + 1))
                if needed(b):
                    pe.wait_ge(L3["x3"].sem, L3["x3"].after(b))
                for j in range(K):
                    i = nc.tensor.matmul(ps[0:p, DC + j * P:DC + (j + 1) * P], fT[u][:, j, 0:p], wd2s[:, :],
                                         start=True, stop=True)
                i.then_inc(L3["d2"].sem, 1)
            node_loop(pe, (dec_turn, 0), (dec_hidden, 1), (dec_out, 2))
            end_phase(pe, PE)

            def z_turn(p):
                pe.wait_ge(A3["h"].sem, A3["h"].after(p.q + 1))
                if needed(p.q - 1):
                    pe.wait_ge(A3["trc"].sem, A3["trc"].after(p.q - 1))
                for c in range(2):
                    o = p.w * 512 + c * P
                    i = nc.tensor.transpose(ps[:, o:o + P], g[:, p.k, c, :], ident[:, :])
                i.then_inc(A3["tr"].sem, 1)

            def z_mm(p):
                pe.wait_ge(A3["trc"].sem, A3["trc"].after(p.q + 1))
                if needed(p.q - 1):
                    pe.wait_ge(A3["z"].sem, A3["z"].after(p.q - 1))
                for c in range(2):
                    o = SUMS + p.w * 512 + c * P
                    i = nc.tensor.matmul(ps[:, o:o + P], xT[:, p.w, c * P:(c + 1) * P], wft[:, :], start=True, stop=True)
                i.then_inc(A3["mm"].sem, 1)
            pair_loop(pe, (z_turn, 0), (z_mm, 0))
            end_phase(pe, PE)
            for n, kind in enumerate(TURNS):
                pe.wait_ge(M3["ready"].sem, M3["ready"].after(n + 1))
                if kind == "row":
                    nc.tensor.transpose(ps[0:1, 0:P], col[:, n:n + 1], ident[:, :]).then_inc(M3["pe"].sem, 1)
                else:
                    nc.tensor.transpose(ps[:, 0:1], names["turned"], ident[0:1, 0:1]).then_inc(M3["pe"].sem, 1)
            end_phase(pe, PE)

            def mul_ready(p):
                pe.wait_ge(B3["mul"].sem, B3["mul"].after(p.q + 1))
            edge_tensor(pe, B3, D, mul_ready, msg, 2)
            end_phase(pe, PE)

        @block.scalar
        def _(a):
            a.wait_ge(S0["deg"].sem, S0["deg"].after(NDEG))
            nc.scalar.activation(dis[0][:, :], dis[0][:, :], ACT.Sqrt).then_inc(S0["root"].sem, 1)
            end_phase(a, AC)
            ln_scalar(a, A0)
            end_phase(a, AC)

            def e0_sums(p):
                sums_out(a, E0, p, tot, D)
            pair_loop(a, (e0_sums, 0))
            a.wait_ge(C0["v"].sem, C0["v"].after(1))
            nc.scalar.activation(dis[1][:, :], dis[1][:, :], ACT.Sqrt).then_inc(C0["root"].sem, 1)
            end_phase(a, AC)

            def turned(signal, b, p, out_t, n, ready, free, func=ACT.Copy, bias=0.0):
                a.wait_ge(ready.sem, ready.after(b + 1))
                if needed(b - SLOTS + 1):
                    a.wait_ge(free.sem, free.after(b - SLOTS + 1))
                nc.scalar.activation(out_t[:, 0:n, 0:p], ps[:, 0:n * P].rearrange("f (k p) -> f k p", p=P)[:, :, 0:p],
                                     func, bias=bias).then_inc(signal.sem, 1)

            def conv0_first(r, u, p):
                b = r * SLOTS + u
                turned(L0["trc"], b, p, fT[u], K, L0["tr"], L0["mm"])
                a.wait_ge(L0["sc"].sem, L0["sc"].after(b + 1))
                a.wait_ge(L0["ld"][u].sem, L0["ld"][u].after(r * 16 + 16))
                if needed(b - SLOTS + 1):
                    a.wait_ge(L0["res"].sem, L0["res"].after(b - SLOTS + 1))
                relu_rows(a, p, ob_h[u], xin[u], sc[:, u, :], nbi[:, u, :]).then_inc(L0["h"].sem, 1)

            def conv0_h1(r, u, p):
                b = r * SLOTS + u
                a.wait_ge(L0["nb"].sem, L0["nb"].after(b + 1))
                if needed(r * 32):
                    a.wait_ge(L0["sto"][u].sem, L0["sto"][u].after(r * 32))
                relu_rows(a, p, hb[u], oa[u], sc2[:, u, :], nb2[:, u, :]).then_inc(L0["h1"].sem, 1)

            def conv0_root(r, u, p):
                root(a, L0, r * SLOTS + u, p)
            node_loop(a, (conv0_first, 0), (conv0_h1, 2), (conv0_root, 1))
            end_phase(a, AC)

            def turned_out(p):
                if needed(p.q - 1):
                    a.wait_ge(E1["masked"].sem, E1["masked"].after(p.q - 1))
                a.wait_ge(E1["tx"].sem, E1["tx"].after(p.q + 1))
                nc.scalar.activation(xT[:, p.w, :], ps[:, TURN[p.w]:TURN[p.w] + 4 * P], ACT.Copy) \
                    .then_inc(E1["txc"].sem, 1)
            turned_out(Pair(0, 0))
            turned_out(Pair(0, 1))

            def e1_body(p):
                turned_out(p.plus(2))
                if needed(p.q - 1):
                    a.wait_ge(E1["mm"].sem, E1["mm"].after(p.q - 1))
                a.wait_ge(E1["xw"].sem, E1["xw"].after(p.q + 1))
                nc.scalar.activation(msg[:, p.w, :, :], pair_of(XW + p.w * 512), ACT.Relu).then_inc(E1["relu"].sem, 1)
                sums_out(a, E1, p, tot, D)
            pair_loop(a, (e1_body, 0))
            end_phase(a, AC)

            def e2_root(p):
                edge_root(a, E2, p, 2)

            def e2_body(p):
                if needed(p.q - 1):
                    a.wait_ge(E2["mm"].sem, E2["mm"].after(p.q - 1))
                edge_relu(a, E2, p, [(msg[:, p.w, c, :], g[:, p.k, c, :]) for c in range(2)], esc)
                sums_out(a, E2, p, tot, D)
            pair_loop(a, (e2_root, 0), (e2_body, 1))
            end_phase(a, AC)

            def enc_first(r, u, p):
                turned(L2["trc"], r * SLOTS + u, p, fT[u], K, L2["tr"], L2["mm"])

            def enc_relu(r, u, p):
                b = r * SLOTS + u
                a.wait_ge(L2["mm"].sem, L2["mm"].after(b + 1))
                if needed(b - SLOTS + 1):
                    a.wait_ge(L2["mm2"].sem, L2["mm2"].after(b - SLOTS + 1))
                nc.scalar.activation(tT[u][:, :, 0:p], zc_view[:, :, 0:p], ACT.Relu, bias=be1c[:, :]) \
                    .then_inc(L2["relu"].sem, 1)

            def enc_h(r, u, p):
                b = r * SLOTS + u
                a.wait_ge(L2["nb"].sem, L2["nb"].after(b + 1))
                relu_rows(a, p, xin[u], xin[u], sc[:, u, :], nbi[:, u, :]).then_inc(L2["h"].sem, 1)

            def enc_root(r, u, p):
                root(a, L2, r * SLOTS + u, p)
            node_loop(a, (enc_root, 0), (enc_first, 3), (enc_relu, 4), (enc_h, 0))
            end_phase(a, AC)

            def e3_sums(p):
                sums_out(a, E3, p, toty, H2)
            pair_loop(a, (e3_sums, 0))
            end_phase(a, AC)

            def dec_first(r, u, p):
                b = r * SLOTS + u
                turned(L3["trc"], b, p, tT[u], K // 2, L3["tr"], L3["d1"], ACT.Relu, be2c[:, :])

            def dec_z3(r, u, p):
                b = r * SLOTS + u
                a.wait_ge(L3["d1"].sem, L3["d1"].after(b + 1))
                if needed(b - SLOTS + 1):
                    a.wait_ge(L3["d2"].sem, L3["d2"].after(b - SLOTS + 1))
                nc.scalar.activation(fT[u][:, :, 0:p], hid_view[:, :, 0:p], ACT.Relu, bias=bd1c[:, :]) \
                    .then_inc(L3["d1c"].sem, 1)

            node_loop(a, (dec_first, 0), (dec_z3, 1))
            end_phase(a, AC)

            def z_turned(p):
                a.wait_ge(A3["tr"].sem, A3["tr"].after(p.q + 1))
                if needed(p.q - 1):
                    a.wait_ge(A3["mm"].sem, A3["mm"].after(p.q - 1))
                nc.scalar.activation(xT[:, p.w, 0:2 * P], ps[:, p.w * 512:p.w * 512 + 2 * P], ACT.Copy) \
                    .then_inc(A3["trc"].sem, 1)

            def z_out(p):
                a.wait_ge(A3["mm"].sem, A3["mm"].after(p.q + 1))
                if needed(p.n):
                    a.wait_ge(A3["sto"][p.k].sem, A3["sto"][p.k].after(p.n * 16))
                    a.wait_ge(A3["e"].sem, A3["e"].after(p.q - RING + 1))
                nc.scalar.activation(tot[:, p.k, :, :], pair_of(SUMS + p.w * 512), ACT.Copy).then_inc(A3["z"].sem, 1)

            def score_root(p):
                edge_root(a, A3, p, 4)

            def score_relu(p):
                edge_relu(a, A3, p, [(t[:, p.k, c, :],) * 2 for t in (g, gd) for c in range(2)], ers)
            pair_loop(a, (score_root, 0), (score_relu, 1), (z_turned, 1), (z_out, 2))
            end_phase(a, AC)
            a.wait_ge(M3["diff"].sem, M3["diff"].after(1))
            nc.scalar.activation(wgt[:, :], wgt[:, :], ACT.Exp).then_inc(M3["exp"].sem, 1)
            end_phase(a, AC)

            def weigh(p):
                a.wait_ge(B3["ring"].sem, B3["ring"].after(p.q + 1))
                if needed(p.q - 1):
                    a.wait_ge(B3["mm"].sem, B3["mm"].after(p.q - 1))
                a.wait_ge(B3["load"][p.k].sem, B3["load"][p.k].after(p.n * 16 + 16))
                for c in range(2):
                    i = nc.scalar.activation(msg[:, p.w, c, :], g[:, p.k, c, :], ACT.Copy, scale=alr[:, p.k, c:c + 1])
                i.then_inc(B3["mul"].sem, 1)

            def b3_sums(p):
                sums_out(a, B3, p, tot, D)
            pair_loop(a, (weigh, 0), (b3_sums, 1))
            end_phase(a, AC)


_INS = ["x", "src", "dst", "edge_attr_32", "edge_type_8", "L0_gnn_W", "L0_gnn_b", "L1_gnn_weight", "L1_gnn_bias",
        "L2_gnn_W_enc1", "L2_gnn_b_enc1", "L2_gnn_W_enc2", "L2_gnn_b_enc2", "L2_gnn_W_dec1", "L2_gnn_b_dec1",
        "L2_gnn_W_dec2", "L2_gnn_b_dec2", "L3_gnn_W_fc", "L3_gnn_W_attn"]


def kernel(**inputs):
    import numpy as _np
    import concourse.bacc as _bacc
    from concourse import mybir as _mybir
    from concourse.bass_utils import run_bass_kernel_spmd as _run

    nc = _bacc.Bacc("TRN2", target_bir_lowering=False, num_devices=1)
    arrays, args = {}, []
    for name in _INS:
        a = _np.ascontiguousarray(inputs[name])
        arrays[f"in_{name}"] = a
        args.append(nc.dram_tensor(f"in_{name}", a.shape, _mybir.dt.from_np(a.dtype), kind="ExternalInput").ap())
    args.append(nc.dram_tensor("out_rows", (NR, D), _mybir.dt.float32, kind="ExternalOutput").ap())
    gnn(nc, *args)
    r = _run(nc, [arrays], core_ids=[0])
    return r.results[0]["out_rows"][:N]
```
